# Optimizing a Trainium2 kernel written in Bass

```python
import numpy as np
import jax
import jax.numpy as jnp

def _softmax(x, axis=-1):
    return jax.nn.softmax(x, axis=axis)

def _gelu(x):
    return jax.nn.gelu(x, approximate=True)

def _silu(x):
    return jax.nn.silu(x)

def _sigmoid(x):
    return jax.nn.sigmoid(x)

def _layernorm(x, axis=-1, eps=1e-05):
    m = jnp.mean(x, axis=axis, keepdims=True)
    v = jnp.var(x, axis=axis, keepdims=True)
    return (x - m) / jnp.sqrt(v + eps)

def _scatter_add(tgt, idx, src, axis=0):
    return tgt.at[idx].add(src)

def _segment_sum(src, seg, n):
    return jax.ops.segment_sum(src, seg, n)
kernel_name = 'mk_adj_ffn_d1_adj_r2_b0073f'

def setup_inputs(seed: int=0):
    np.random.seed(seed)
    _w = jnp.asarray

    def _rec_inputs():
        import jax
        import jax.numpy as jnp
        _gk = jax.random.key(seed)
        x = -0.0002928 + 1 * jax.random.normal(jax.random.fold_in(_gk, 1), (128, 128, 128), jnp.float32)
        _a = jax.random.bernoulli(jax.random.fold_in(_gk, 2), 0.0625, (128, 128, 128))
        _a = jnp.logical_or(_a, jnp.swapaxes(_a, -1, -2))
        _a = jnp.logical_or(_a, jnp.eye(128, dtype=bool))
        _af = _a.astype(jnp.float32)
        _af = _af * jax.random.uniform(jax.random.fold_in(_gk, 3), (128, 128, 128), jnp.float32, 0.05, 1)
        adj = _af
        return (x, adj)
    x, adj = _rec_inputs()

    def _L0_gnn_setup():
        import jax, jax.numpy as jnp
        import numpy as np
        B, N, D, H = (8, 1024, 128, 512)
        RMS_EPS = 1e-06

        def _rmsnorm(h, w, eps=RMS_EPS):
            var = jnp.mean(jnp.square(h), axis=-1, keepdims=True)
            return h * jax.lax.rsqrt(var + eps) * w
        key = jax.random.key(seed)
        ks = jax.random.split(key, 5)
        x = jax.random.normal(ks[0], (B, N, D), dtype=jnp.float32)
        adjacency = jax.random.uniform(ks[1], (B, N, N), dtype=jnp.float32)
        epsilon = jnp.zeros((), dtype=jnp.float32)
        W1 = jax.random.normal(ks[2], (D, H), dtype=jnp.float32) * (1.0 / np.sqrt(D))
        b1 = jnp.zeros((H,), dtype=jnp.float32)
        rms_weight = jnp.ones((H,), dtype=jnp.float32)
        W2 = jax.random.normal(ks[3], (H, D), dtype=jnp.float32) * (1.0 / np.sqrt(H))
        b2 = jnp.zeros((D,), dtype=jnp.float32)
        return {'x': x, 'adjacency': adjacency, 'epsilon': epsilon, 'W1': W1, 'b1': b1, 'rms_weight': rms_weight, 'W2': W2, 'b2': b2}
    _L0_gnn_all = _L0_gnn_setup()
    _L0_gnn_in = {k: v for k, v in _L0_gnn_all.items() if k in ('epsilon', 'W1', 'b1', 'rms_weight', 'W2', 'b2')}
    del _L0_gnn_all

    def _L0_ffn_setup():
        import jax, jax.numpy as jnp
        import numpy as np
        B, S, H, F, E, K = (8, 2048, 128, 256, 16, 2)
        EPS = 1e-05
        key = jax.random.key(seed)
        ks = jax.random.split(key, 9)
        sc = 0.02
        return {'x': jax.random.normal(ks[0], (B, S, H), dtype=jnp.float32), 'gate_w': jax.random.normal(ks[1], (H, E), dtype=jnp.float32) * sc, 'gate_b': jnp.zeros((E,), dtype=jnp.float32), 'w1': jax.random.normal(ks[2], (E, H, F), dtype=jnp.float32) * sc, 'b1': jnp.zeros((E, F), dtype=jnp.float32), 'w2': jax.random.normal(ks[3], (E, F, H), dtype=jnp.float32) * sc, 'b2': jnp.zeros((E, H), dtype=jnp.float32), 'gamma': jnp.ones((H,), dtype=jnp.float32), 'beta': jnp.zeros((H,), dtype=jnp.float32)}
    _L0_ffn_all = _L0_ffn_setup()
    _L0_ffn_in = {k: v for k, v in _L0_ffn_all.items() if k in ('gate_w', 'gate_b', 'w1', 'b1', 'w2', 'b2', 'gamma', 'beta')}
    del _L0_ffn_all
    return {'x': x, 'adj': adj, 'L0_gnn_epsilon': _L0_gnn_in['epsilon'], 'L0_gnn_W1': _L0_gnn_in['W1'], 'L0_gnn_b1': _L0_gnn_in['b1'], 'L0_gnn_rms_weight': _L0_gnn_in['rms_weight'], 'L0_gnn_W2': _L0_gnn_in['W2'], 'L0_gnn_b2': _L0_gnn_in['b2'], 'L0_ffn_gate_w': _L0_ffn_in['gate_w'], 'L0_ffn_gate_b': _L0_ffn_in['gate_b'], 'L0_ffn_w1': _L0_ffn_in['w1'], 'L0_ffn_b1': _L0_ffn_in['b1'], 'L0_ffn_w2': _L0_ffn_in['w2'], 'L0_ffn_b2': _L0_ffn_in['b2'], 'L0_ffn_gamma': _L0_ffn_in['gamma'], 'L0_ffn_beta': _L0_ffn_in['beta']}

def reference(x, adj, L0_gnn_epsilon, L0_gnn_W1, L0_gnn_b1, L0_gnn_rms_weight, L0_gnn_W2, L0_gnn_b2, L0_ffn_gate_w, L0_ffn_gate_b, L0_ffn_w1, L0_ffn_b1, L0_ffn_w2, L0_ffn_b2, L0_ffn_gamma, L0_ffn_beta):
    import jax
    import jax.numpy as jnp

    def _L0_gnn_ref(x, adjacency, epsilon, W1, b1, rms_weight, W2, b2):
        import jax, jax.numpy as jnp
        import numpy as np
        B, N, D, H = (8, 1024, 128, 512)
        RMS_EPS = 1e-06

        def _rmsnorm(h, w, eps=RMS_EPS):
            var = jnp.mean(jnp.square(h), axis=-1, keepdims=True)
            return h * jax.lax.rsqrt(var + eps) * w
        neighbor_sum = jnp.einsum('bnm,bmd->bnd', adjacency, x)
        agg = epsilon * x + neighbor_sum
        h = jnp.einsum('bnd,dh->bnh', agg, W1) + b1
        h = jax.nn.silu(_rmsnorm(h, rms_weight))
        out = jnp.einsum('bnh,hd->bnd', h, W2) + b2
        return out

    def _L0_ffn_ref(x, gate_w, gate_b, w1, b1, w2, b2, gamma, beta):
        import jax, jax.numpy as jnp
        import numpy as np
        B, S, H, F, E, K = (8, 2048, 128, 256, 16, 2)
        EPS = 1e-05
        gate_logits = x @ gate_w + gate_b
        topk_vals, topk_idx = jax.lax.top_k(gate_logits, K)
        topk_w = jax.nn.softmax(topk_vals, axis=-1)
        h = jax.nn.relu(jnp.einsum('bsh,ehf->bsef', x, w1) + b1)
        expert_out = jnp.einsum('bsef,efh->bseh', h, w2) + b2
        sel = jnp.take_along_axis(expert_out, topk_idx[:, :, :, None], axis=2)
        moe = jnp.sum(topk_w[..., None] * sel, axis=2)
        y = x + moe
        mu = jnp.mean(y, axis=-1, keepdims=True)
        var = jnp.var(y, axis=-1, keepdims=True)
        return (y - mu) / jnp.sqrt(var + EPS) * gamma + beta
    x = x + _L0_gnn_ref(_layernorm(x, axis=-1), adj, L0_gnn_epsilon, L0_gnn_W1, L0_gnn_b1, L0_gnn_rms_weight, L0_gnn_W2, L0_gnn_b2)
    x = x + _L0_ffn_ref(_layernorm(x, axis=-1), L0_ffn_gate_w, L0_ffn_gate_b, L0_ffn_w1, L0_ffn_b1, L0_ffn_w2, L0_ffn_b2, L0_ffn_gamma, L0_ffn_beta)
    return x

_drawn_inputs = setup_inputs


def setup_inputs(seed=0):
    import zlib

    import numpy as np

    out = dict(_drawn_inputs(seed))
    spreads = {'L0_gnn_b1': (0.0, 0.302),
     'L0_gnn_rms_weight': (1.0, 0.2),
     'L0_gnn_b2': (0.0, 0.1),
     'L0_ffn_gate_b': (0.0, 0.268),
     'L0_ffn_b1': (0.0, 0.8),
     'L0_ffn_b2': (0.0, 0.281),
     'L0_ffn_gamma': (1.0, 0.2),
     'L0_ffn_beta': (0.0, 0.1)}
    factors = {'L0_ffn_w1': 3.958, 'L0_ffn_w2': 3.116}
    for name, (base, spread) in spreads.items():
        noise = np.random.default_rng([zlib.crc32(name.encode()), seed]).standard_normal(out[name].shape)
        drawn = base * np.exp(spread * noise) if base else spread * noise
        out[name] = jnp.asarray(drawn.astype(out[name].dtype))
    for name, factor in factors.items():
        out[name] = (out[name] * factor).astype(out[name].dtype)
    return out
```

```python
import concourse.bass as bass
from concourse import mybir
from contextlib import ExitStack

P = 128
NB = 128
GB = 4
NG = NB // GB
D = 128
H = 512
HC = H // P
E = 16
TOPK = 2
F = 256
FC = F // P
TOK = NB * P
ROW = D + 4
TILE = 256
TH = TILE // P
CAP = TOK + TILE
NT = TOK * TOPK // TILE + E - 1
WROW = F + FC * D + FC + D
SKIP = 1 << 20
RING = 3
RING2 = 4
LN_EPS = 1e-5
RMS_EPS = 1e-6


def gnn_moe(nc, x, adj_t, eps, w1, b1, rms_w, w2, b2, gate_w, gate_b, w_exp, gamma, beta, out):
    fp32, bf16, i32, u32 = mybir.dt.float32, mybir.dt.bfloat16, mybir.dt.int32, mybir.dt.uint32
    ALU, ACT, AX = mybir.AluOpType, mybir.ActivationFunctionType, mybir.AxisListType

    dispatched = nc.dram_tensor("dispatched", [(E + 1) * CAP, ROW], fp32, kind="Internal").ap()
    combined = nc.dram_tensor("combined", [TOK * TOPK, D], fp32, kind="Internal").ap()
    combined_by_node = combined.rearrange("(n b k) d -> n b k d", n=P, k=TOPK)

    ctx = ExitStack()
    with ctx:
        def sb(name, shape, dt=fp32):
            return ctx.enter_context(nc.sbuf_tensor(name, shape, dt))

        def sem(name):
            return ctx.enter_context(nc.semaphore(name))

        def ring_of(name, n):
            return [sem(f"{name}{k}") for k in range(n)]

        ident = sb("ident", [P, P])
        eps_ident = sb("eps_ident", [P, P])
        ones_f = sb("ones_f", [P, 1])
        ones_b = sb("ones_b", [P, P], bf16)
        before = sb("before", [P, P], bf16)
        upto = sb("upto", [P, E, E])
        neg_half = sb("neg_half", [P, P])
        iota_e = sb("iota_e", [P, E], i32)
        base_i = sb("base_i", [P, E], i32)
        base_e = sb("base_e", [P, E])
        iota_ti = sb("iota_ti", [1, NT], i32)
        iota_t = sb("iota_t", [1, NT])
        eps_sb = sb("eps_sb", [P, 1])
        w1_sb = sb("w1_sb", [P, H])
        w2_sb = sb("w2_sb", [P, HC, D])
        b1_sb = sb("b1_sb", [P, HC])
        rms_sb = sb("rms_sb", [P, HC])
        b2_sb = sb("b2_sb", [P, D])
        gw_sb = sb("gw_sb", [P, E])
        gb_sb = sb("gb_sb", [P, E])
        gamma_sb = sb("gamma_sb", [P, D])
        beta_sb = sb("beta_sb", [P, D])

        xs = sb("xs", [P, NB, D])
        adj_sb = sb("adj_sb", [P, RING, GB, P])
        bn = sb("bn", [P, 2, RING, GB, 6])
        mv = sb("mv", [P, 2, RING, GB, 2])
        ve = sb("ve", [P, 2, RING, GB])
        rstd = sb("rstd", [P, 2, RING, GB])
        nb = sb("nb", [P, 2, RING, GB])
        mv_all = sb("mv_all", [P, NB, 2])
        xn = sb("xn", [P, GB, D])
        agg = sb("agg", [P, GB * P])
        work = sb("work", [P, 3, HC, GB * P])
        sq, zbuf, sbuf_s = work[:, 0], work[:, 1], work[:, 2]
        sq_sum = sb("sq_sum", [P, 3, GB * P])
        ms = sb("ms", [P, GB])
        rms = sb("rms", [P, GB])
        rms_b = sb("rms_b", [P, GB * P])
        rows = sb("rows", [P, RING, GB, TOPK, ROW])
        ut = sb("ut", [P, GB * P])
        lgs = sb("lgs", [P, GB, E])
        top_v = sb("top_v", [P, GB, 8])
        top_i = sb("top_i", [P, GB, 8], u32)
        hot = sb("hot", [P, GB, TOPK, E])
        cnt = sb("cnt", [P, RING, GB, E], bf16)
        carry = sb("carry", [P, RING, GB, E], bf16)
        slot_e = sb("slot_e", [P, GB, E])
        slot_m = sb("slot_m", [P, GB, TOPK, E])
        slot_f = sb("slot_f", [P, GB * TOPK])
        slot_i = sb("slot_i", [P, RING, GB * TOPK], i32)
        gap_all = sb("gap_all", [P, NB])
        tot = sb("tot", [P, E])
        nt_i = sb("nt_i", [P, 2, E], i32)
        nt_f = sb("nt_f", [P, E])
        nt_m = sb("nt_m", [P, E, E])
        end_t = sb("end_t", [P, E])
        room = work[:, :, :, :].rearrange("p a b c -> p (a b c)")
        t_m = room[0:1, 0:NT * E].rearrange("p (t e) -> p t e", e=E)
        t_n = room[0:1, NT * E:2 * NT * E].rearrange("p (t e) -> p t e", e=E)
        t_e = sb("t_e", [1, NT])
        t_s = sb("t_s", [1, NT])
        t_r = sb("t_r", [1, 4, NT])
        table = sb("table", [1, 2, NT], i32)
        pad_f = sb("pad_f", [1, E])
        pad_row = sb("pad_row", [1, E], i32)
        pad = sb("pad", [P, TH, ROW])
        ve_all = sb("ve_all", [P, NB])
        rstd_all = sb("rstd_all", [P, NB])
        nb_all = sb("nb_all", [P, NB])
        gw_e = sb("gw_e", [P, NB])
        gw_d = sb("gw_d", [P, NB])
        gate = sb("gate", [P, TOPK, NB])
        tin = sb("tin", [P, RING2, TH, ROW])
        wts = sb("wts", [P, RING2, WROW])
        tut = sb("tut", [P, 2, TILE])
        hid = sb("hid", [P, 2, FC, TILE])
        tout = sb("tout", [P, RING2, TH, D])
        moe = sb("moe", [P, RING, GB, TOPK, D])
        u3, y3, n3, xb3 = (room[:, k * RING * GB * D:(k + 1) * RING * GB * D]
                           .rearrange("p (k j d) -> p k j d", k=RING, j=GB) for k in range(4))
        g3 = sb("g3", [P, RING, GB, D])
        o3 = sb("o3", [P, RING, GB, D])

        bank = [ctx.enter_context(nc.psum_tensor(f"bank{k}", [P, 512], fp32)) for k in range(8)]
        h_ps, agg_ps, out_ps, rb_ps, misc_ps = bank[0:4], bank[4], bank[5], bank[6], bank[7]
        tut_ps, hid_ps, exp_ps = bank[0:2], bank[2:4], bank[4:6]

        consts = sem("consts")
        made = sem("made")
        ini = sem("ini")
        made2 = sem("made2")
        loaded = ring_of("loaded", RING)
        bn_done = [sem("bn1_done"), sem("bn2_done")]
        mv_done = [sem("mv1_done"), sem("mv2_done")]
        ve_done = [sem("ve1_done"), sem("ve2_done")]
        rstd_done = [sem("rstd1_done"), sem("rstd2_done")]
        nb_done = [sem("nb1_done"), sem("nb2_done")]
        mv_kept = sem("mv_kept")
        xn_done = sem("xn_done")
        xb_done = sem("xb_done")
        agg_done = sem("agg_done")
        agg_out = sem("agg_out")
        h_done = sem("h_done")
        sq_done = sem("sq_done")
        half_done = sem("half_done")
        sum_done = sem("sum_done")
        ms_done = sem("ms_done")
        ms_out = sem("ms_out")
        rms_done = sem("rms_done")
        rb_done = sem("rb_done")
        rb_out = sem("rb_out")
        z_done = sem("z_done")
        s_done = sem("s_done")
        out_done = sem("out_done")
        x1_done = sem("x1_done")
        u_done = sem("u_done")
        ut_done = sem("ut_done")
        ut_out = sem("ut_out")
        lg_done = sem("lg_done")
        lg_out = sem("lg_out")
        topv_done = sem("topv_done")
        topi_done = sem("topi_done")
        hot_done = sem("hot_done")
        cnt_done = sem("cnt_done")
        carry_done = sem("carry_done")
        gap_done = sem("gap_done")
        rank_done = sem("rank_done")
        slote_done = sem("slote_done")
        slotm_done = sem("slotm_done")
        slotf_done = sem("slotf_done")
        slot_done = sem("slot_done")
        dest_done = sem("dest_done")
        scattered = ring_of("scattered", RING)
        tot_done = sem("tot_done")
        tab = sem("tab")
        table_done = sem("table_done")
        gate_done = sem("gate_done")
        exp_done = sem("exp_done")
        all_rstd = sem("all_rstd")
        all_nb = sem("all_nb")
        padded = sem("padded")
        tin_in = ring_of("tin_in", RING2)
        wts_in = ring_of("wts_in", RING2)
        t_tr = sem("t_tr")
        t_ut = sem("t_ut")
        t_h = sem("t_h")
        t_relu = sem("t_relu")
        t_o = sem("t_o")
        t_out = sem("t_out")
        t_scat = ring_of("t_scat", RING2)
        moe_in = ring_of("moe_in", RING)
        p_u = sem("p_u")
        p_y1 = sem("p_y1")
        p_y = sem("p_y")
        p_bn = sem("p_bn")
        p_mv = sem("p_mv")
        p_ve = sem("p_ve")
        p_rs = sem("p_rs")
        p_nb = sem("p_nb")
        p_n = sem("p_n")
        p_g = sem("p_g")
        p_xb = sem("p_xb")
        p_o = sem("p_o")
        stored = ring_of("stored", RING)

        def count(i, n, per=1, each=RING):
            return per * n if i is None else i * (per * each) + per * n

        def has(i, g, n=NG):
            return i is not None or 0 <= g < n

        def pipeline(eng, step, first, lead, turns, last, each=RING):
            for t in range(first, lead):
                step(None, t)
            with eng.Fori(0, turns) as i:
                for k in range(each):
                    step(i, lead + k)
            for t in range(lead + turns * each, last):
                step(None, t)

        P1 = (-2, 6, (NG - 2 - 6) // RING, NG + 4)
        P2 = (-1, 5, (NT - 1 - 5) // RING2, NT + 1)
        P3 = (0, 6, (NG - 6) // RING, NG + 3)

        N_CONST = 13
        N_MADE = 12

        block = ctx.enter_context(nc.Block())

        @block.sync
        def _(sp):
            for dst, src in (
                (w1_sb[:], w1), (w2_sb[:], w2), (b1_sb[:], b1), (rms_sb[:], rms_w),
                (gw_sb[:], gate_w),
                (eps_sb[:], eps.partition_broadcast(P)), (b2_sb[:], b2.partition_broadcast(P)),
                (gb_sb[:], gate_b.partition_broadcast(P)), (gamma_sb[:], gamma.partition_broadcast(P)),
                (beta_sb[:], beta.partition_broadcast(P)),
            ):
                sp.dma_start(dst, src).then_inc(consts, 16)

            def step(i, t):
                g = t + 3
                if has(i, g):
                    k = g % RING
                    if g >= RING:
                        sp.wait_ge(agg_done, count(i, g - RING + 1))
                    b = count(i, g, GB)
                    sp.dma_start(xs[:, bass.ds(b, GB), :], x[:, bass.ds(b, GB), :]).then_inc(loaded[k], 16)
                    sp.dma_start(adj_sb[:, k], adj_t[:, bass.ds(b, GB), :]).then_inc(loaded[k], 16)

            pipeline(sp, step, -3, 3, (NG - 6) // RING, NG)

            sp.wait_ge(table_done, 1)
            sp.wait_ge(made2, 2)
            pad_rows = lambda r: dispatched[bass.ds(r, TILE), :].rearrange("(p a) w -> p a w", a=TH)
            sp.dma_start(pad_rows(E * CAP), pad[:]).then_inc(padded, 16)
            for e in range(E):
                r = sp.value_load(pad_row[0:1, e:e + 1], min_val=0, max_val=E * CAP)
                sp.dma_start(pad_rows(r), pad[:]).then_inc(padded, 16)
            sp.wait_ge(padded, 16 * (E + 1))
            for k in range(RING):
                sp.wait_ge(scattered[k], 16 * GB * TOPK * len(range(k, NG, RING)))

            def tile_step(i, t):
                n = t + 2
                if has(i, n, NT):
                    k = n % RING2
                    at = count(i, n, 1, RING2)
                    r = sp.value_load(table[0:1, 0, bass.ds(at, 1)], min_val=0, max_val=E * CAP)
                    w = sp.value_load(table[0:1, 1, bass.ds(at, 1)], min_val=0, max_val=(E - 1) * P)
                    if n >= RING2:
                        sp.wait_ge(t_scat[k], count(i, n // RING2, 16 * TH, 1))
                    sp.dma_start(tin[:, k], dispatched[bass.ds(r, TILE), :].rearrange("(a p) w -> p a w", p=P))\
                        .then_inc(tin_in[k], 16)
                    if n >= RING2:
                        sp.wait_ge(t_out, count(i, n - RING2 + 1, 1, RING2))
                    sp.dma_start(wts[:, k], w_exp[bass.ds(w, P), :]).then_inc(wts_in[k], 16)

            pipeline(sp, tile_step, -2, 2, (NT - 4) // RING2, NT, RING2)
            for k in range(RING2):
                sp.wait_ge(t_scat[k], 16 * TH * len(range(k, NT, RING2)))

            def post_step(i, t):
                g = t
                if has(i, g):
                    k = g % RING
                    if g >= RING:
                        sp.wait_ge(p_y, count(i, g - RING + 1))
                    sp.dma_start(moe[:, k], combined_by_node[:, bass.ds(count(i, g, GB), GB)])\
                        .then_inc(moe_in[k], 16)
                g = t - 3
                if has(i, g):
                    k = g % RING
                    sp.wait_ge(p_o, count(i, g + 1))
                    sp.dma_start(out[:, bass.ds(count(i, g, GB), GB), :], o3[:, k]).then_inc(stored[k], 16)

            pipeline(sp, post_step, *P3)
            for k in range(RING):
                sp.wait_ge(stored[k], 16 * len(range(k, NG, RING)))

        @block.gpsimd
        def _(pool):
            nc.gpsimd.memset(ident[:], 0.0).then_inc(ini, 1)
            nc.gpsimd.memset(before[:], 1.0).then_inc(ini, 1)
            nc.gpsimd.memset(upto[:], 1.0).then_inc(ini, 1)
            nc.gpsimd.memset(ones_f[:], 1.0).then_inc(made, 1)
            nc.gpsimd.memset(ones_b[:], 1.0).then_inc(made, 1)
            nc.gpsimd.memset(neg_half[:], -0.5).then_inc(made, 1)
            nc.gpsimd.memset(carry[:, 0], 0.0).then_inc(made, 1)
            nc.gpsimd.iota(iota_e[:], pattern=[[1, E]], base=0, channel_multiplier=0).then_inc(made, 1)
            nc.gpsimd.iota(base_i[:], pattern=[[CAP, E]], base=0, channel_multiplier=0).then_inc(made, 1)
            nc.gpsimd.iota(iota_ti[:], pattern=[[1, NT]], base=0, channel_multiplier=0).then_inc(made, 1)
            nc.gpsimd.memset(rows[:], 0.0).then_inc(ini, 1)
            nc.gpsimd.memset(pad[:], 0.0).then_inc(ini, 1)
            pool.wait_ge(ini, 5)
            nc.gpsimd.affine_select(out=ident[:], in_=ident[:], compare_op=ALU.not_equal, fill=1.0, base=0,
                                    pattern=[[-1, P]], channel_multiplier=1).then_inc(made, 1)
            nc.gpsimd.affine_select(out=before[:], in_=before[:], compare_op=ALU.is_gt, fill=0.0, base=0,
                                    pattern=[[1, P]], channel_multiplier=-1).then_inc(made, 1)
            nc.gpsimd.affine_select(out=upto[:], in_=upto[:], compare_op=ALU.is_ge, fill=0.0, base=0,
                                    pattern=[[1, E], [-1, E]], channel_multiplier=0).then_inc(made, 1)
            for k in range(RING):
                nc.gpsimd.iota(rows[:, k, :, :, D:D + 1].bitcast(i32).rearrange("p b c o -> p (b c) o"),
                               pattern=[[1, GB * TOPK], [1, 1]], base=(k - RING) * GB * TOPK,
                               channel_multiplier=NB * TOPK).then_inc(made2 if k == 0 else made, 1)
            nc.gpsimd.iota(pad[:, :, D:D + 1].bitcast(i32), pattern=[[0, TH], [0, 1]], base=SKIP,
                           channel_multiplier=0).then_inc(made2, 1)
            pool.wait_ge(made, N_MADE)

            def power(ln, i, g):
                k = g % RING
                pool.wait_ge(ve_done[ln], count(i, g + 1))
                nc.gpsimd.tensor_tensor(rstd[:, ln, k], ve[:, ln, k], neg_half[:, 0:GB], ALU.pow)\
                    .then_inc(rstd_done[ln], 1)

            def dispatch(i, g, part):
                k = g % RING
                if part[0] == 0:
                    pool.wait_ge(slot_done, count(i, g + 1))
                    pool.wait_ge(dest_done, count(i, g + 1))
                    pool.nop(nofuse=True)
                for n in part:
                    nc.gpsimd.indirect_dma_start(
                        dispatched, bass.IndirectOffsetOnAxis(slot_i[:, k, n:n + 1], 0),
                        rows[:, k, n // TOPK, n % TOPK, :], None).then_inc(scattered[k], 16)

            def step(i, t):
                if has(i, t - 2):
                    power(1, i, t - 2)
                if has(i, t - 4):
                    dispatch(i, t - 4, (0, 1, 2))
                if has(i, t + 2):
                    power(0, i, t + 2)
                if has(i, t):
                    pool.wait_ge(ms_out, count(i, t + 1))
                    nc.gpsimd.tensor_tensor(rms[:], ms[:], neg_half[:, 0:GB], ALU.pow).then_inc(rms_done, 1)
                if has(i, t - 4):
                    dispatch(i, t - 4, (3, 4, 5, 6, 7))

            pipeline(pool, step, *P1)

            pool.wait_ge(all_rstd, 1)
            nc.gpsimd.tensor_tensor(rstd_all[:], ve_all[:], neg_half[:, 0:NB], ALU.pow).then_inc(all_rstd, 1)

            def tile_step(i, t):
                n = t - 1
                if has(i, n, NT):
                    k = n % RING2
                    pool.wait_ge(t_out, count(i, n + 1, 1, RING2))
                    pool.nop(nofuse=True)
                    for a in range(TH):
                        nc.gpsimd.indirect_dma_start(
                            combined, bass.IndirectOffsetOnAxis(tin[:, k, a, D:D + 1].bitcast(i32), 0),
                            tout[:, k, a, :], None, bounds_check=TOK * TOPK - 1, oob_is_err=False)\
                            .then_inc(t_scat[k], 16)

            pipeline(pool, tile_step, *P2, RING2)

            def post_step(i, t):
                g = t - 1
                if has(i, g):
                    k = g % RING
                    pool.wait_ge(p_ve, count(i, g + 1))
                    nc.gpsimd.tensor_tensor(rstd[:, 0, k], ve[:, 0, k], neg_half[:, 0:GB], ALU.pow)\
                        .then_inc(p_rs, 1)
                g = t - 2
                if has(i, g):
                    k = g % RING
                    pool.wait_ge(p_n, count(i, g + 1))
                    nc.gpsimd.tensor_tensor(g3[:, k], n3[:, k],
                                            gamma_sb[:, :].unsqueeze(1).broadcast_to([P, GB, D]),
                                            ALU.mult).then_inc(p_g, 1)
                g = t
                if has(i, g):
                    k = g % RING
                    if g >= RING:
                        pool.wait_ge(p_o, count(i, g - RING + 1))
                        pool.nop(nofuse=True)
                    nc.gpsimd.tensor_tensor(
                        xb3[:, k], xs[:, bass.ds(count(i, g, GB), GB), :],
                        beta_sb[:, :].unsqueeze(1).broadcast_to([P, GB, D]), ALU.add).then_inc(p_xb, 1)

            pipeline(pool, post_step, *P3)

        @block.tensor
        def _(pe):
            pe.wait_ge(consts, 16 * 10)
            pe.wait_ge(made, N_MADE)
            pe.wait_ge(made2, 3)

            def out_layer(g, graphs):
                for j in graphs:
                    for c in range(HC):
                        last = nc.tensor.matmul(out_ps[:, j * D:(j + 1) * D],
                                                sbuf_s[:, c, j * P:(j + 1) * P], w2_sb[:, c, :],
                                                start=(c == 0), stop=(c == HC - 1))
                return last

            def step(i, t):
                g = t
                if has(i, g):
                    pe.wait_ge(agg_out, count(i, g + 1))
                    for c in range(HC):
                        if g >= 1:
                            pe.wait_ge(z_done, count(i, HC * (g - 1) + c + 1, 1, RING * HC))
                        nc.tensor.matmul(h_ps[c][:, :], w1_sb[:, c * P:(c + 1) * P], agg[:],
                                         start=True, stop=True).then_inc(h_done, 1)
                g = t - 3
                if has(i, g):
                    k = g % RING
                    pe.wait_ge(u_done, count(i, g + 1))
                    if g >= 1:
                        pe.wait_ge(slote_done, count(i, g))
                    for j in range(GB):
                        last = nc.tensor.transpose(misc_ps[:, j * P:(j + 1) * P], rows[:, k, j, 0, 0:D],
                                                   ident[:])
                    last.then_inc(ut_done, 1)
                g = t - 1
                if has(i, g):
                    pe.wait_ge(s_done, count(i, HC * (g + 1), 1, RING * HC))
                    if g >= 1:
                        pe.wait_ge(x1_done, count(i, g))
                    out_layer(g, (0, 1))
                g = t
                if has(i, g):
                    pe.wait_ge(sum_done, count(i, g + 1))
                    for j in range(GB):
                        last = nc.tensor.matmul(agg_ps[:, j:j + 1], sq_sum[:, 2, j * P:(j + 1) * P],
                                                ones_f[:], start=True, stop=True)
                    last.then_inc(ms_done, 1)
                g = t - 3
                if has(i, g):
                    pe.wait_ge(ut_out, count(i, g + 1))
                    for j in range(GB):
                        last = nc.tensor.matmul(misc_ps[:, j * E:(j + 1) * E], ut[:, j * P:(j + 1) * P],
                                                gw_sb[:], start=True, stop=True)
                    last.then_inc(lg_done, 1)
                g = t - 1
                if has(i, g):
                    out_layer(g, (2,))
                g = t
                if has(i, g):
                    pe.wait_ge(rms_done, count(i, g + 1))
                    for j in range(GB):
                        last = nc.tensor.matmul(rb_ps[:, j * P:(j + 1) * P],
                                                rms[:, j:j + 1].broadcast_to([P, P]), ident[:],
                                                start=True, stop=True)
                    last.then_inc(rb_done, 1)
                g = t - 1
                if has(i, g):
                    out_layer(g, (3,)).then_inc(out_done, 1)
                g = t + 1
                if has(i, g):
                    k = g % RING
                    pe.wait_ge(loaded[k], count(i, g // RING + 1, 32, 1))
                    pe.wait_ge(xn_done, count(i, g + 1))
                    if g >= 1:
                        pe.wait_ge(ms_out, count(i, g))
                    for j in range(GB):
                        nc.tensor.matmul(agg_ps[:, j * P:(j + 1) * P], xn[:, j, :], adj_sb[:, k, j, :],
                                         start=True, stop=False)
                        last = nc.tensor.matmul(agg_ps[:, j * P:(j + 1) * P], xn[:, j, :], eps_ident[:],
                                                start=False, stop=True)
                    last.then_inc(agg_done, 1)
                g = t - 3
                if has(i, g):
                    k = g % RING
                    pe.wait_ge(cnt_done, count(i, g + 1))
                    if g >= 1:
                        pe.wait_ge(carry_done, count(i, g))
                    wide = lambda a, n: a.unsqueeze(1).broadcast_to([P, n, E])
                    nc.tensor.matmul(misc_ps[:, 0:GB * E], before[:],
                                     cnt[:, k].rearrange("p j e -> p (j e)"), start=True, stop=False)
                    for j in range(GB - 1):
                        nc.tensor.matmul(misc_ps[:, (j + 1) * E:GB * E].rearrange("p (j e) -> p j e", e=E),
                                         ones_b[:], wide(cnt[:, k, j, :], GB - 1 - j), start=False, stop=False)
                    for j in range(GB):
                        last = nc.tensor.matmul(misc_ps[:, 0:GB * E].rearrange("p (j e) -> p j e", e=E),
                                                ones_b[:], wide(carry[:, k, j, :], GB), start=False,
                                                stop=(j == GB - 1))
                    last.then_inc(rank_done, 1)

            pipeline(pe, step, *P1)

            pe.wait_ge(carry_done, NG)
            pe.wait_ge(slote_done, NG)
            for j in range(GB):
                last = nc.tensor.matmul(misc_ps[:, 0:E], ones_b[:], carry[:, NG % RING, j, :],
                                        start=(j == 0), stop=(j == GB - 1))
            last.then_inc(tot_done, 1)

            def tile_step(i, t):
                n = t + 1
                if has(i, n, NT):
                    k = n % RING2
                    pe.wait_ge(tin_in[k], count(i, n // RING2 + 1, 16, 1))
                    if n >= 2:
                        pe.wait_ge(t_ut, count(i, n - 1, 1, RING2))
                    for a in range(TH):
                        last = nc.tensor.transpose(tut_ps[n % 2][:, a * P:(a + 1) * P], tin[:, k, a, 0:D],
                                                   ident[:])
                    last.then_inc(t_tr, 1)
                n = t
                if has(i, n, NT):
                    k = n % RING2
                    pe.wait_ge(wts_in[k], count(i, n // RING2 + 1, 16, 1))
                    pe.wait_ge(t_ut, count(i, n + 1, 1, RING2))
                    if n >= 2:
                        pe.wait_ge(t_relu, count(i, n - 1, 1, RING2))
                    for c in range(FC):
                        last = nc.tensor.matmul(hid_ps[n % 2][:, c * TILE:(c + 1) * TILE],
                                                wts[:, k, c * P:(c + 1) * P], tut[:, n % 2, :],
                                                start=True, stop=True)
                    last.then_inc(t_h, 1)
                n = t - 1
                if has(i, n, NT):
                    k = n % RING2
                    pe.wait_ge(t_relu, count(i, n + 1, 1, RING2))
                    if n >= 2:
                        pe.wait_ge(t_out, count(i, n - 1, 1, RING2))
                    for a in range(TH):
                        for c in range(FC):
                            last = nc.tensor.matmul(exp_ps[n % 2][:, a * D:(a + 1) * D],
                                                    hid[:, n % 2, c, a * P:(a + 1) * P],
                                                    wts[:, k, F + c * D:F + (c + 1) * D],
                                                    start=(c == 0), stop=(c == FC - 1))
                    last.then_inc(t_o, 1)

            pe.wait_ge(x1_done, NG)
            pipeline(pe, tile_step, *P2, RING2)

        @block.scalar
        def _(act):
            def step(i, t):
                g = t
                if has(i, g):
                    act.wait_ge(agg_done, count(i, g + 1))
                    nc.scalar.activation(agg[:], agg_ps[:, :], ACT.Copy).then_inc(agg_out, 1)
                g = t - 1
                if has(i, g):
                    if g >= 1:
                        act.wait_ge(out_done, count(i, g))
                    for c in range(HC):
                        act.wait_ge(z_done, count(i, HC * g + c + 1, 1, RING * HC))
                        nc.scalar.activation(sbuf_s[:, c, :], zbuf[:, c, :], ACT.Silu,
                                             scale=rms_sb[:, c:c + 1]).then_inc(s_done, 1)
                g = t
                if has(i, g):
                    if g == 0 and i is None:
                        act.wait_ge(consts, 16 * 10)
                    for c in range(HC):
                        act.wait_ge(h_done, count(i, HC * g + c + 1, 1, RING * HC))
                        nc.scalar.activation(sq[:, c, :], h_ps[c][:, :], ACT.Square, bias=b1_sb[:, c:c + 1])\
                            .then_inc(sq_done, 1)
                g = t - 3
                if has(i, g):
                    act.wait_ge(ut_done, count(i, g + 1))
                    nc.scalar.activation(ut[:], misc_ps[:, :], ACT.Copy).then_inc(ut_out, 1)
                g = t - 2
                if has(i, g):
                    k = g % RING
                    if g >= RING:
                        act.wait_ge(scattered[k], count(i, g // RING, 16 * GB * TOPK, 1))
                    act.wait_ge(nb_done[1], count(i, g + 1))
                    act.nop(nofuse=True)
                    for j in range(GB):
                        last = nc.scalar.activation(
                            rows[:, k, j, :, 0:D],
                            xs[:, bass.ds(count(i, g, GB) + j, 1), :].broadcast_to([P, TOPK, D]),
                            ACT.Identity, bias=nb[:, 1, k, j:j + 1], scale=rstd[:, 1, k, j:j + 1])
                    last.then_inc(u_done, 1)
                g = t
                if has(i, g):
                    act.wait_ge(rb_done, count(i, g + 1))
                    nc.scalar.activation(rms_b[:], rb_ps[:, :], ACT.Copy).then_inc(rb_out, 1)

            pipeline(act, step, *P1)

            act.wait_ge(gap_done, NG)
            nc.scalar.activation(gw_e[:], gap_all[:], ACT.Exp).then_inc(exp_done, 1)

            def tile_step(i, t):
                n = t
                if has(i, n, NT):
                    k = n % RING2
                    if n >= 2:
                        act.wait_ge(t_o, count(i, n - 1, 1, RING2))
                    act.wait_ge(t_h, count(i, n + 1, 1, RING2))
                    for c in range(FC):
                        last = nc.scalar.activation(
                            hid[:, n % 2, c, :], hid_ps[n % 2][:, c * TILE:(c + 1) * TILE], ACT.Relu,
                            bias=wts[:, k, F + FC * D + c:F + FC * D + c + 1])
                    last.then_inc(t_relu, 1)

            act.wait_ge(wts_in[0], 16)
            pipeline(act, tile_step, *P2, RING2)

            act.wait_ge(all_nb, 1)

            def post_step(i, t):
                g = t
                if has(i, g):
                    k = g % RING
                    if g >= RING:
                        act.wait_ge(p_y, count(i, g - RING + 1))
                        act.nop(nofuse=True)
                    for j in range(GB):
                        b = count(i, g, GB) + j
                        last = nc.scalar.activation(
                            u3[:, k, j, :], xs[:, bass.ds(b, 1), :].rearrange("p o d -> p (o d)"),
                            ACT.Identity, bias=nb_all[:, bass.ds(b, 1)], scale=rstd_all[:, bass.ds(b, 1)])
                    last.then_inc(p_u, 1)
                g = t - 2
                if has(i, g):
                    k = g % RING
                    act.wait_ge(p_nb, count(i, g + 1))
                    act.nop(nofuse=True)
                    for j in range(GB):
                        last = nc.scalar.activation(n3[:, k, j, :], y3[:, k, j, :], ACT.Identity,
                                                    bias=nb[:, 0, k, j:j + 1], scale=rstd[:, 0, k, j:j + 1])
                    last.then_inc(p_n, 1)

            pipeline(act, post_step, *P3)

        @block.vector
        def _(dve):
            dve.wait_ge(made, N_MADE)
            dve.wait_ge(consts, 16 * 10)
            nc.vector.tensor_scalar(eps_ident[:], ident[:], eps_sb[:, 0:1], None, ALU.mult).then_inc(made2, 1)
            nc.vector.tensor_copy(base_e[:], base_i[:]).then_inc(tab, 1)
            nc.vector.tensor_copy(iota_t[:], iota_ti[:]).then_inc(tab, 1)
            dve.wait_ge(tab, 2)

            def variance(ln, i, g):
                k = g % RING
                dve.wait_ge(bn_done[ln], count(i, g + 1))
                dve.nop(nofuse=True)
                for j in range(GB):
                    last = nc.vector.bn_aggr(mv[:, ln, k, j, :], bn[:, ln, k, j, :])
                last.then_inc(mv_done[ln], 1)

            def variance_eps(ln, i, g):
                k = g % RING
                dve.wait_ge(mv_done[ln], count(i, g + 1))
                nc.vector.tensor_scalar(ve[:, ln, k], mv[:, ln, k, :, 1], LN_EPS, None, ALU.add)\
                    .then_inc(ve_done[ln], 1)

            def offset(ln, i, g):
                k = g % RING
                dve.wait_ge(rstd_done[ln], count(i, g + 1))
                nc.vector.scalar_tensor_tensor(out=nb[:, ln, k], in0=mv[:, ln, k, :, 0], scalar=-1.0,
                                               in1=rstd[:, ln, k], op0=ALU.mult, op1=ALU.mult)\
                    .then_inc(nb_done[ln], 1)

            def step(i, t):
                g = t - 2
                if has(i, g):
                    k = g % RING
                    x1 = xs[:, bass.ds(count(i, g, GB), GB), :]
                    dve.wait_ge(out_done, count(i, g + 1))
                    nc.vector.tensor_tensor(x1, out_ps[:, :].rearrange("p (b d) -> p b d", d=D), x1,
                                            ALU.add).then_inc(x1_done, 1)
                    dve.wait_ge(x1_done, count(i, g + 1))
                    dve.nop(nofuse=True)
                    for j in range(GB):
                        last = nc.vector.bn_stats(bn[:, 1, k, j, :], xs[:, bass.ds(count(i, g, GB) + j, 1), :])
                    last.then_inc(bn_done[1], 1)
                g = t + 2
                if has(i, g):
                    k = g % RING
                    dve.wait_ge(loaded[k], count(i, g // RING + 1, 32, 1))
                    dve.nop(nofuse=True)
                    for j in range(GB):
                        last = nc.vector.bn_stats(bn[:, 0, k, j, :], xs[:, bass.ds(count(i, g, GB) + j, 1), :])
                    last.then_inc(bn_done[0], 1)
                if has(i, t - 2):
                    variance(1, i, t - 2)
                if has(i, t + 2):
                    variance(0, i, t + 2)
                if has(i, t - 2):
                    variance_eps(1, i, t - 2)
                    nc.vector.tensor_copy(mv_all[:, bass.ds(count(i, t - 2, GB), GB), :], mv[:, 1, (t - 2) % RING])\
                        .then_inc(mv_kept, 1)
                if has(i, t + 2):
                    variance_eps(0, i, t + 2)
                g = t + 1
                if has(i, g):
                    k = g % RING
                    offset(0, i, g)
                    if g >= 1:
                        dve.wait_ge(agg_done, count(i, g))
                    dve.wait_ge(nb_done[0], count(i, g + 1))
                    for j in range(GB):
                        last = nc.vector.tensor_scalar(
                            xn[:, j, :], xs[:, bass.ds(count(i, g, GB) + j, 1), :].rearrange("p o d -> p (o d)"),
                            rstd[:, 0, k, j:j + 1], nb[:, 0, k, j:j + 1], ALU.mult, ALU.add)
                    last.then_inc(xn_done, 1)
                if has(i, t - 2):
                    offset(1, i, t - 2)
                g = t + 1
                if has(i, g):
                    xb = xs[:, bass.ds(count(i, g, GB), GB), :]
                    dve.wait_ge(xn_done, count(i, g + 1))
                    nc.vector.tensor_tensor(xb, xb, b2_sb[:, :].unsqueeze(1).broadcast_to([P, GB, D]), ALU.add)\
                        .then_inc(xb_done, 1)
                g = t
                if has(i, g):
                    for n in range(2):
                        dve.wait_ge(sq_done, count(i, HC * g + 2 * n + 2, 1, RING * HC))
                        nc.vector.tensor_tensor(sq_sum[:, n, :], sq[:, 2 * n, :], sq[:, 2 * n + 1, :], ALU.add)\
                            .then_inc(half_done, 1)
                    dve.wait_ge(half_done, count(i, 2 * g + 2, 1, 2 * RING))
                    nc.vector.tensor_tensor(sq_sum[:, 2, :], sq_sum[:, 0, :], sq_sum[:, 1, :], ALU.add)\
                        .then_inc(sum_done, 1)
                    dve.wait_ge(ms_done, count(i, g + 1))
                    nc.vector.tensor_scalar(ms[:], agg_ps[:, 0:GB], 1.0 / H, RMS_EPS, ALU.mult, ALU.add)\
                        .then_inc(ms_out, 1)
                g = t - 3
                if has(i, g):
                    k = g % RING
                    dve.wait_ge(lg_done, count(i, g + 1))
                    nc.vector.tensor_tensor(lgs[:], misc_ps[:, 0:GB * E].rearrange("p (j e) -> p j e", e=E),
                                            gb_sb[:, :].unsqueeze(1).broadcast_to([P, GB, E]), ALU.add)\
                        .then_inc(lg_out, 1)
                    dve.wait_ge(lg_out, count(i, g + 1))
                    dve.nop(nofuse=True)
                    for j in range(GB):
                        last = nc.vector.max(top_v[:, j, :], lgs[:, j, :])
                    last.then_inc(topv_done, 1)
                    dve.wait_ge(topv_done, count(i, g + 1))
                    dve.nop(nofuse=True)
                    for j in range(GB):
                        last = nc.vector.max_index(top_i[:, j, :], top_v[:, j, :], lgs[:, j, :])
                    last.then_inc(topi_done, 1)
                    nc.vector.tensor_tensor(gap_all[:, bass.ds(count(i, g, GB), GB)], top_v[:, :, 1],
                                            top_v[:, :, 0], ALU.subtract).then_inc(gap_done, 1)
                    dve.wait_ge(topi_done, count(i, g + 1))
                    for c in range(TOPK):
                        last = nc.vector.tensor_tensor(
                            hot[:, :, c, :], iota_e[:, :].unsqueeze(1).broadcast_to([P, GB, E]),
                            top_i[:, :, c:c + 1].broadcast_to([P, GB, E]), ALU.is_equal)
                    last.then_inc(hot_done, 1)
                    dve.wait_ge(hot_done, count(i, g + 1))
                    nc.vector.tensor_tensor(cnt[:, k], hot[:, :, 0, :], hot[:, :, 1, :], ALU.add)\
                        .then_inc(cnt_done, 1)
                    dve.wait_ge(cnt_done, count(i, g + 1))
                    nc.vector.tensor_tensor(carry[:, (k + 1) % RING], carry[:, k], cnt[:, k], ALU.add)\
                        .then_inc(carry_done, 1)
                g = t
                if has(i, g):
                    dve.wait_ge(rb_out, count(i, g + 1))
                    for c in range(HC):
                        nc.vector.scalar_tensor_tensor(out=zbuf[:, c, :], in0=h_ps[c][:, :],
                                                       scalar=b1_sb[:, c:c + 1], in1=rms_b[:],
                                                       op0=ALU.add, op1=ALU.mult).then_inc(z_done, 1)
                g = t - 3
                if has(i, g):
                    k = g % RING
                    dve.wait_ge(rank_done, count(i, g + 1))
                    nc.vector.tensor_tensor(slot_e[:], misc_ps[:, 0:GB * E].rearrange("p (j e) -> p j e", e=E),
                                            base_e[:, :].unsqueeze(1).broadcast_to([P, GB, E]), ALU.add)\
                        .then_inc(slote_done, 1)
                    dve.wait_ge(slote_done, count(i, g + 1))
                    for c in range(TOPK):
                        last = nc.vector.tensor_tensor(slot_m[:, :, c, :], hot[:, :, c, :], slot_e[:], ALU.mult)
                    last.then_inc(slotm_done, 1)
                    if g >= RING:
                        dve.wait_ge(scattered[k], count(i, g // RING, 16 * GB * TOPK, 1))
                    dest = rows[:, k, :, :, D:D + 1].bitcast(i32).rearrange("p b c o -> p (b c) o")
                    nc.vector.tensor_scalar(dest, dest, float(RING * GB * TOPK), None, ALU.add)\
                        .then_inc(dest_done, 1)
                    dve.wait_ge(slotm_done, count(i, g + 1))
                    nc.vector.tensor_reduce(slot_f[:], slot_m[:].rearrange("p j c e -> p (j c) e"),
                                            axis=AX.X, op=ALU.add).then_inc(slotf_done, 1)
                    dve.wait_ge(slotf_done, count(i, g + 1))
                    nc.vector.tensor_copy(slot_i[:, k, :], slot_f[:]).then_inc(slot_done, 1)

            pipeline(dve, step, *P1)

            n = [2]

            def link(ins):
                n[0] += 1
                ins.then_inc(tab, 1)
                dve.wait_ge(tab, n[0])

            dve.wait_ge(mv_kept, NG)
            nc.vector.tensor_scalar(ve_all[:], mv_all[:, :, 1], LN_EPS, None, ALU.add).then_inc(all_rstd, 1)

            dve.wait_ge(tot_done, 1)
            link(nc.vector.tensor_copy(tot[:], misc_ps[:, 0:E]))
            link(nc.vector.tensor_scalar(nt_i[:, 0, :], tot[:], float(TILE - 1), None, ALU.add))
            link(nc.vector.tensor_single_scalar(nt_i[:, 1, :], nt_i[:, 0, :], TILE.bit_length() - 1,
                                                op=ALU.arith_shift_right))
            link(nc.vector.tensor_copy(nt_f[:], nt_i[:, 1, :]))
            link(nc.vector.tensor_tensor(nt_m[:], upto[:], nt_f[:, :].unsqueeze(1).broadcast_to([P, E, E]),
                                         ALU.mult))
            link(nc.vector.tensor_reduce(end_t[:], nt_m[:], axis=AX.X, op=ALU.add))
            link(nc.vector.tensor_tensor(t_m[:], end_t[0:1, :].unsqueeze(1).broadcast_to([1, NT, E]),
                                         iota_t[:, :].unsqueeze(2).broadcast_to([1, NT, E]), ALU.is_le))
            link(nc.vector.tensor_reduce(t_e[:], t_m[:], axis=AX.X, op=ALU.add))
            link(nc.vector.tensor_tensor(t_n[:], t_m[:], nt_f[0:1, :].unsqueeze(1).broadcast_to([1, NT, E]),
                                         ALU.mult))
            link(nc.vector.tensor_reduce(t_s[:], t_n[:], axis=AX.X, op=ALU.add))
            link(nc.vector.tensor_tensor(t_r[:, 0], iota_t[:], t_s[:], ALU.subtract))
            link(nc.vector.tensor_scalar(t_r[:, 1], t_e[:], float(CAP), None, ALU.mult))
            link(nc.vector.scalar_tensor_tensor(out=t_r[:, 2], in0=t_r[:, 0], scalar=float(TILE),
                                                in1=t_r[:, 1], op0=ALU.mult, op1=ALU.add))
            link(nc.vector.tensor_scalar(table[:, 0], t_r[:, 2], float(E * CAP), None, ALU.min))
            link(nc.vector.tensor_scalar(table[:, 1], t_e[:], float(E - 1), float(P), ALU.min, ALU.mult))
            link(nc.vector.tensor_tensor(pad_row[:], base_e[0:1, :], tot[0:1, :], ALU.add))
            nc.vector.tensor_copy(pad_f[:], pad_row[:]).then_inc(table_done, 1)

            dve.wait_ge(exp_done, 1)
            link(nc.vector.tensor_scalar(gw_d[:], gw_e[:], 1.0, None, ALU.add))
            link(nc.vector.reciprocal(gate[:, 0, :], gw_d[:]))
            link(nc.vector.tensor_tensor(gate[:, 1, :], gw_e[:], gate[:, 0, :], ALU.mult))
            dve.wait_ge(all_rstd, 2)
            nc.vector.scalar_tensor_tensor(out=nb_all[:], in0=mv_all[:, :, 0], scalar=-1.0, in1=rstd_all[:],
                                           op0=ALU.mult, op1=ALU.mult).then_inc(all_nb, 1)

            def tile_step(i, t):
                n = t + 1
                if has(i, n, NT):
                    dve.wait_ge(t_tr, count(i, n + 1, 1, RING2))
                    if n >= 2:
                        dve.wait_ge(t_h, count(i, n - 1, 1, RING2))
                    nc.vector.tensor_copy(tut[:, n % 2, :], tut_ps[n % 2][:, 0:TILE]).then_inc(t_ut, 1)
                n = t - 1
                if has(i, n, NT):
                    k = n % RING2
                    if n >= RING2:
                        dve.wait_ge(t_scat[k], count(i, n // RING2, 16 * TH, 1))
                    dve.wait_ge(t_o, count(i, n + 1, 1, RING2))
                    nc.vector.tensor_tensor(
                        tout[:, k], exp_ps[n % 2][:, 0:TH * D].rearrange("p (a d) -> p a d", d=D),
                        wts[:, k, WROW - D:WROW].unsqueeze(1).broadcast_to([P, TH, D]), ALU.add)\
                        .then_inc(t_out, 1)

            pipeline(dve, tile_step, *P2, RING2)

            def post_step(i, t):
                g = t
                if has(i, g):
                    k = g % RING
                    dve.wait_ge(p_u, count(i, g + 1))
                    dve.wait_ge(moe_in[k], count(i, g // RING + 1, 16, 1))
                    for j in range(GB):
                        last = nc.vector.scalar_tensor_tensor(
                            out=u3[:, k, j, :], in0=moe[:, k, j, 0, :],
                            scalar=gate[:, 0, bass.ds(count(i, g, GB) + j, 1)],
                            in1=u3[:, k, j, :], op0=ALU.mult, op1=ALU.add)
                    last.then_inc(p_y1, 1)
                    dve.wait_ge(p_y1, count(i, g + 1))
                    for j in range(GB):
                        last = nc.vector.scalar_tensor_tensor(
                            out=y3[:, k, j, :], in0=moe[:, k, j, 1, :],
                            scalar=gate[:, 1, bass.ds(count(i, g, GB) + j, 1)],
                            in1=u3[:, k, j, :], op0=ALU.mult, op1=ALU.add)
                    last.then_inc(p_y, 1)
                    last = None
                    dve.wait_ge(p_y, count(i, g + 1))
                    for j in range(GB):
                        last = nc.vector.bn_stats(bn[:, 0, k, j, :], y3[:, k, j, :])
                    last.then_inc(p_bn, 1)
                    dve.wait_ge(p_bn, count(i, g + 1))
                    dve.nop(nofuse=True)
                    for j in range(GB):
                        last = nc.vector.bn_aggr(mv[:, 0, k, j, :], bn[:, 0, k, j, :])
                    last.then_inc(p_mv, 1)
                    dve.wait_ge(p_mv, count(i, g + 1))
                    nc.vector.tensor_scalar(ve[:, 0, k], mv[:, 0, k, :, 1], LN_EPS, None, ALU.add)\
                        .then_inc(p_ve, 1)
                g = t - 1
                if has(i, g):
                    k = g % RING
                    dve.wait_ge(p_rs, count(i, g + 1))
                    nc.vector.scalar_tensor_tensor(out=nb[:, 0, k], in0=mv[:, 0, k, :, 0], scalar=-1.0,
                                                   in1=rstd[:, 0, k], op0=ALU.mult, op1=ALU.mult)\
                        .then_inc(p_nb, 1)
                g = t - 3
                if has(i, g):
                    k = g % RING
                    if g >= RING:
                        dve.wait_ge(stored[k], count(i, g // RING, 16, 1))
                    dve.wait_ge(p_xb, count(i, g + 1))
                    dve.wait_ge(p_g, count(i, g + 1))
                    nc.vector.tensor_tensor(o3[:, k], g3[:, k], xb3[:, k], ALU.add).then_inc(p_o, 1)

            pipeline(dve, post_step, *P3)


def kernel(**inputs):
    import numpy as np
    import concourse.bacc as bacc
    from concourse.bass_utils import run_bass_kernel_spmd

    a = {k: np.asarray(v) for k, v in inputs.items()}
    col = lambda v, n: np.ascontiguousarray(v.reshape(n, P).T)
    w_exp = np.concatenate([
        a["L0_ffn_w1"],
        a["L0_ffn_w2"].reshape(E, FC, P, D).transpose(0, 2, 1, 3).reshape(E, P, FC * D),
        a["L0_ffn_b1"].reshape(E, FC, P).transpose(0, 2, 1),
        np.broadcast_to(a["L0_ffn_b2"][:, None, :], (E, P, D)),
    ], axis=2).reshape(E * P, WROW)
    arrays = {
        "x": a["x"].transpose(1, 0, 2),
        "adj_t": a["adj"].transpose(2, 0, 1),
        "eps": a["L0_gnn_epsilon"].reshape(1),
        "w1": a["L0_gnn_W1"], "b1": col(a["L0_gnn_b1"], HC), "rms_w": col(a["L0_gnn_rms_weight"], HC),
        "w2": a["L0_gnn_W2"].reshape(HC, P, D).transpose(1, 0, 2), "b2": a["L0_gnn_b2"],
        "gate_w": a["L0_ffn_gate_w"], "gate_b": a["L0_ffn_gate_b"],
        "w_exp": w_exp, "gamma": a["L0_ffn_gamma"], "beta": a["L0_ffn_beta"],
    }
    arrays = {k: np.ascontiguousarray(v) for k, v in arrays.items()}
    nc = bacc.Bacc("TRN2", target_bir_lowering=False, num_devices=1)
    args = [nc.dram_tensor(f"in_{k}", v.shape, mybir.dt.from_np(v.dtype), kind="ExternalInput").ap()
            for k, v in arrays.items()]
    out = nc.dram_tensor("out_0", (P, NB, D), mybir.dt.float32, kind="ExternalOutput").ap()
    gnn_moe(nc, *args, out)
    r = run_bass_kernel_spmd(nc, [{f"in_{k}": v for k, v in arrays.items()}], core_ids=[0])
    return np.ascontiguousarray(r.results[0]["out_0"].transpose(1, 0, 2))
```

```python
import concourse.bass as bass
from concourse import mybir
from contextlib import ExitStack

P = 128
NB = 128
GB = 4
NG = NB // GB
D = 128
H = 512
HC = H // P
E = 16
TOPK = 2
F = 256
FC = F // P
TOK = NB * P
ROW = D + 4
TILE = 256
TH = TILE // P
CAP = TOK + TILE
NT = TOK * TOPK // TILE + E - 1
WROW = F + FC * D + FC + D
SKIP = 1 << 20
RING = 3
RING2 = 6
LN_EPS = 1e-5
RMS_EPS = 1e-6


def gnn_moe(nc, x, adj_t, eps, w1, b1, rms_w, w2, b2, gate_w, gate_b, w_exp, gamma, beta, out):
    fp32, bf16, i32, u32 = mybir.dt.float32, mybir.dt.bfloat16, mybir.dt.int32, mybir.dt.uint32
    ALU, ACT, AX = mybir.AluOpType, mybir.ActivationFunctionType, mybir.AxisListType

    dispatched = nc.dram_tensor("dispatched", [(E + 1) * CAP, ROW], fp32, kind="Internal").ap()
    combined = nc.dram_tensor("combined", [TOK * TOPK, D], fp32, kind="Internal").ap()
    combined_by_node = combined.rearrange("(n b k) d -> n b k d", n=P, k=TOPK)

    ctx = ExitStack()
    with ctx:
        def sb(name, shape, dt=fp32):
            return ctx.enter_context(nc.sbuf_tensor(name, shape, dt))

        def sem(name):
            return ctx.enter_context(nc.semaphore(name))

        def ring_of(name, n):
            return [sem(f"{name}{k}") for k in range(n)]

        ident = sb("ident", [P, P])
        eps_ident = sb("eps_ident", [P, P])
        ones_f = sb("ones_f", [P, 1])
        ones_b = sb("ones_b", [P, P], bf16)
        before = sb("before", [P, P], bf16)
        upto = sb("upto", [P, E, E])
        neg_half = sb("neg_half", [P, 2 * GB])
        iota_e = sb("iota_e", [P, E], i32)
        base_i = sb("base_i", [P, E], i32)
        base_e = sb("base_e", [P, E])
        iota_ti = sb("iota_ti", [1, NT], i32)
        iota_t = sb("iota_t", [1, NT])
        eps_sb = sb("eps_sb", [P, 1])
        w1_sb = sb("w1_sb", [P, H])
        w2_sb = sb("w2_sb", [P, HC, D])
        b1_sb = sb("b1_sb", [P, HC])
        rms_sb = sb("rms_sb", [P, HC])
        b2_sb = sb("b2_sb", [3, D])
        b2_rest = sb("b2_rest", [3, 2, D])
        b2_part = sb("b2_part", [3, 3, D], bf16)
        b2_row = sb("b2_row", [3, 3, D], bf16)
        b2_parts = sb("b2_parts", [3, GB * D], bf16)
        gw_sb = sb("gw_sb", [P, E])
        gb_sb = sb("gb_sb", [P, E])
        gamma_sb = sb("gamma_sb", [P, D])
        beta_sb = sb("beta_sb", [P, D])

        xs = sb("xs", [P, NB, D])
        adj_sb = sb("adj_sb", [P, RING, GB, P])
        bn = sb("bn", [P, 2, RING, GB, 6])
        mv = sb("mv", [P, 2, RING, GB, 2])
        ve = sb("ve", [P, RING, 2, GB])
        rstd = sb("rstd", [P, RING, 2, GB])
        nb = sb("nb", [P, RING, GB])
        rstd_all = sb("rstd_all", [P, NB])
        nb_all = sb("nb_all", [P, NB])
        xn = sb("xn", [P, GB, D])
        agg = sb("agg", [P, GB * P])
        work = sb("work", [P, 3, HC, GB * P])
        sq, zbuf, sbuf_s = work[:, 0], work[:, 1], work[:, 2]
        sq_sum = sb("sq_sum", [P, 3, GB * P])
        ms = sb("ms", [P, GB])
        rms = sb("rms", [P, GB])
        rms_b = sb("rms_b", [P, GB * P])
        rows = sb("rows", [P, RING, GB, TOPK, ROW])
        ut = sb("ut", [P, GB * P])
        lgs = sb("lgs", [P, GB, E])
        top_v = sb("top_v", [P, GB, 8])
        top_i = sb("top_i", [P, GB, 8], u32)
        hot = sb("hot", [P, GB, TOPK, E])
        cnt = sb("cnt", [P, RING, GB, E], bf16)
        carry = sb("carry", [P, RING, GB, E], bf16)
        slot_e = sb("slot_e", [P, GB, E])
        slot_m = sb("slot_m", [P, GB, TOPK, E])
        slot_f = sb("slot_f", [P, GB * TOPK])
        slot_i = sb("slot_i", [P, RING, GB * TOPK], i32)
        gap_all = sb("gap_all", [P, NB])
        tot = sb("tot", [P, E])
        nt_i = sb("nt_i", [P, 2, E], i32)
        nt_f = sb("nt_f", [P, E])
        nt_m = sb("nt_m", [P, E, E])
        end_t = sb("end_t", [P, E])
        room = work[:, :, :, :].rearrange("p a b c -> p (a b c)")
        t_m = room[0:1, 0:NT * E].rearrange("p (t e) -> p t e", e=E)
        t_n = room[0:1, NT * E:2 * NT * E].rearrange("p (t e) -> p t e", e=E)
        t_e = sb("t_e", [1, NT])
        t_s = sb("t_s", [1, NT])
        t_r = sb("t_r", [1, 4, NT])
        table = sb("table", [1, 2, NT], i32)
        pad_row = sb("pad_row", [1, E], i32)
        pad = sb("pad", [P, TH, ROW])
        gw_e = sb("gw_e", [P, NB])
        gw_d = sb("gw_d", [P, NB])
        gate = sb("gate", [P, TOPK, NB])
        tin = sb("tin", [P, RING2, TH, ROW])
        wts = sb("wts", [P, RING2, WROW])
        tut = sb("tut", [P, 2, TILE])
        hid = sb("hid", [P, 2, FC, TILE])
        tdest = sb("tdest", [P, RING2, TH], i32)
        tout = sb("tout", [P, RING2, TH, D])
        moe = sb("moe", [P, RING, GB, TOPK, D])
        u3, y3, n3, xb3 = (room[:, k * RING * GB * D:(k + 1) * RING * GB * D]
                           .rearrange("p (k j d) -> p k j d", k=RING, j=GB) for k in range(4))
        g3 = sb("g3", [P, RING, GB, D])
        o3 = sb("o3", [P, RING, GB, D])

        bank = [ctx.enter_context(nc.psum_tensor(f"bank{k}", [P, 512], fp32)) for k in range(8)]
        h_ps, agg_ps, out_ps, rb_ps, misc_ps = bank[0:4], bank[4], bank[5], bank[6], bank[7]
        tut_ps, hid_ps, exp_ps = bank[0:2], bank[2:4], bank[4:6]

        consts = sem("consts")
        made = sem("made")
        ini = sem("ini")
        made2 = sem("made2")
        loaded = ring_of("loaded", RING)
        bn_done = [sem("bn1_done"), sem("bn2_done")]
        mv_done = [sem("mv1_done"), sem("mv2_done")]
        ve_done = [sem("ve1_done"), sem("ve2_done")]
        rstd_done = sem("rstd_done")
        nb_done = [sem("nb1_done"), sem("nb2_done")]
        rstd_kept = sem("rstd_kept")
        xn_done = sem("xn_done")
        agg_done = sem("agg_done")
        agg_out = sem("agg_out")
        h_done = sem("h_done")
        sq_done = sem("sq_done")
        half_done = sem("half_done")
        sum_done = sem("sum_done")
        ms_done = sem("ms_done")
        ms_out = sem("ms_out")
        rms_done = sem("rms_done")
        rb_done = sem("rb_done")
        rb_out = sem("rb_out")
        z_done = sem("z_done")
        s_done = sem("s_done")
        out_done = sem("out_done")
        x1_done = sem("x1_done")
        u_done = sem("u_done")
        ut_done = sem("ut_done")
        ut_out = sem("ut_out")
        lg_done = sem("lg_done")
        lg_out = sem("lg_out")
        topv_done = sem("topv_done")
        topi_done = sem("topi_done")
        hot_done = sem("hot_done")
        cnt_done = sem("cnt_done")
        carry_done = sem("carry_done")
        gap_done = sem("gap_done")
        rank_done = sem("rank_done")
        slote_done = sem("slote_done")
        slotm_done = sem("slotm_done")
        slotf_done = sem("slotf_done")
        slot_done = sem("slot_done")
        dest_done = sem("dest_done")
        scattered = ring_of("scattered", RING)
        tot_done = sem("tot_done")
        tab = sem("tab")
        table_done = sem("table_done")
        exp_done = sem("exp_done")
        pad_done = sem("pad_done")
        padded = sem("padded")
        tin_in = ring_of("tin_in", RING2)
        wts_in = ring_of("wts_in", RING2)
        t_tr = sem("t_tr")
        t_ut = sem("t_ut")
        t_h = sem("t_h")
        t_relu = sem("t_relu")
        t_o = sem("t_o")
        t_out = sem("t_out")
        t_scat = ring_of("t_scat", RING2)
        moe_in = ring_of("moe_in", RING)
        p_u = sem("p_u")
        p_y1 = sem("p_y1")
        p_y = sem("p_y")
        p_bn = sem("p_bn")
        p_mv = sem("p_mv")
        p_ve = sem("p_ve")
        p_rs = sem("p_rs")
        p_nb = sem("p_nb")
        p_n = sem("p_n")
        p_g = sem("p_g")
        p_xb = sem("p_xb")
        p_o = sem("p_o")
        stored = ring_of("stored", RING)

        def count(i, n, per=1, each=RING):
            return per * n if i is None else i * (per * each) + per * n

        def has(i, g, n=NG):
            return i is not None or 0 <= g < n

        def pipeline(eng, step, first, lead, turns, last, each=RING):
            for t in range(first, lead):
                step(None, t)
            with eng.Fori(0, turns) as i:
                for k in range(each):
                    step(i, lead + k)
            for t in range(lead + turns * each, last):
                step(None, t)

        P1 = (-2, 6, (NG - 2 - 6) // RING, NG + 4)
        P2 = (-1, 7, (NT - 1 - 7) // RING2, NT + 1)
        P3 = (-2, 7, (NG - 2 - 7) // RING, NG + 4)


        def step_of(ln, g):
            return g - 2 if ln == 0 else g + 2

        N_MADE = 13

        def pad_rows(r):
            return dispatched[bass.ds(r, TILE), :].rearrange("(p a) w -> p a w", a=TH)

        block = ctx.enter_context(nc.Block())

        @block.sync
        def _(sp):
            for dst, src in (
                (w1_sb[:], w1), (w2_sb[:], w2), (b1_sb[:], b1), (rms_sb[:], rms_w),
                (gw_sb[:], gate_w),
                (eps_sb[:], eps.partition_broadcast(P)), (b2_sb[:], b2.partition_broadcast(3)),
                (gb_sb[:], gate_b.partition_broadcast(P)), (gamma_sb[:], gamma.partition_broadcast(P)),
                (beta_sb[:], beta.partition_broadcast(P)),
            ):
                sp.dma_start(dst, src).then_inc(consts, 16)

            def step(i, t):
                g = t + 3
                if has(i, g):
                    k = g % RING
                    if g >= RING:
                        sp.wait_ge(agg_done, count(i, g - RING + 1))
                    b = count(i, g, GB)
                    sp.dma_start(xs[:, bass.ds(b, GB), :], x[:, bass.ds(b, GB), :]).then_inc(loaded[k], 16)
                    sp.dma_start(adj_sb[:, k], adj_t[:, bass.ds(b, GB), :]).then_inc(loaded[k], 16)

            pipeline(sp, step, -3, 3, (NG - 6) // RING, NG)

            sp.wait_ge(made2, 4)
            sp.dma_start(pad_rows(E * CAP), pad[:]).then_inc(padded, 16)
            sp.wait_ge(pad_done, 1)
            for e in range(E // 2):
                r = sp.value_load(pad_row[0:1, e:e + 1], min_val=0, max_val=E * CAP)
                sp.dma_start(pad_rows(r), pad[:]).then_inc(padded, 16)
            sp.wait_ge(padded, 16 * (E + 1))
            sp.wait_ge(table_done, 1)
            for k in range(RING):
                sp.wait_ge(scattered[k], 16 * GB * TOPK * len(range(k, NG, RING)))

            def tile_step(i, t):
                n = t + 4
                if has(i, n, NT):
                    k = n % RING2
                    at = count(i, n, 1, RING2)
                    r = sp.value_load(table[0:1, 0, bass.ds(at, 1)], min_val=0, max_val=E * CAP)
                    if n >= RING2:
                        sp.wait_ge(t_out, count(i, n - RING2 + 1, 1, RING2))
                    sp.dma_start(tin[:, k], dispatched[bass.ds(r, TILE), :].rearrange("(a p) w -> p a w", p=P))\
                        .then_inc(tin_in[k], 16)

            pipeline(sp, tile_step, -4, 2, (NT - 6) // RING2, NT, RING2)
            for k in range(RING2):
                sp.wait_ge(t_scat[k], 16 * TH * len(range(k, NT, RING2)))

            def post_step(i, t):
                g = t + 2
                if has(i, g):
                    k = g % RING
                    if g >= RING:
                        sp.wait_ge(p_y, count(i, g - RING + 1))
                    sp.dma_start(moe[:, k], combined_by_node[:, bass.ds(count(i, g, GB), GB)])\
                        .then_inc(moe_in[k], 16)
                g = t - 4
                if has(i, g):
                    k = g % RING
                    sp.wait_ge(p_o, count(i, g + 1))
                    sp.dma_start(out[:, bass.ds(count(i, g, GB), GB), :], o3[:, k]).then_inc(stored[k], 16)

            pipeline(sp, post_step, *P3)
            for k in range(RING):
                sp.wait_ge(stored[k], 16 * len(range(k, NG, RING)))

        @block.gpsimd
        def _(pool):
            nc.gpsimd.memset(ident[:], 0.0).then_inc(ini, 1)
            nc.gpsimd.memset(before[:], 1.0).then_inc(ini, 1)
            nc.gpsimd.memset(upto[:], 1.0).then_inc(ini, 1)
            nc.gpsimd.memset(ones_f[:], 1.0).then_inc(made, 1)
            nc.gpsimd.memset(ones_b[:], 1.0).then_inc(made, 1)
            nc.gpsimd.memset(neg_half[:], -0.5).then_inc(made, 1)
            nc.gpsimd.memset(carry[:, 0], 0.0).then_inc(made, 1)
            nc.gpsimd.memset(ve[:], 1.0).then_inc(made, 1)
            nc.gpsimd.iota(iota_e[:], pattern=[[1, E]], base=0, channel_multiplier=0).then_inc(made, 1)
            nc.gpsimd.iota(base_i[:], pattern=[[CAP, E]], base=0, channel_multiplier=0).then_inc(made, 1)
            nc.gpsimd.iota(iota_ti[:], pattern=[[1, NT]], base=0, channel_multiplier=0).then_inc(made, 1)
            nc.gpsimd.memset(rows[:], 0.0).then_inc(ini, 1)
            nc.gpsimd.memset(pad[:], 0.0).then_inc(ini, 1)
            pool.wait_ge(ini, 5)
            nc.gpsimd.affine_select(out=ident[:], in_=ident[:], compare_op=ALU.not_equal, fill=1.0, base=0,
                                    pattern=[[-1, P]], channel_multiplier=1).then_inc(made, 1)
            nc.gpsimd.affine_select(out=before[:], in_=before[:], compare_op=ALU.is_gt, fill=0.0, base=0,
                                    pattern=[[1, P]], channel_multiplier=-1).then_inc(made, 1)
            nc.gpsimd.affine_select(out=upto[:], in_=upto[:], compare_op=ALU.is_ge, fill=0.0, base=0,
                                    pattern=[[1, E], [-1, E]], channel_multiplier=0).then_inc(made, 1)
            for k in range(RING):
                nc.gpsimd.iota(rows[:, k, :, :, D:D + 1].bitcast(i32).rearrange("p b c o -> p (b c) o"),
                               pattern=[[1, GB * TOPK], [1, 1]], base=(k - RING) * GB * TOPK,
                               channel_multiplier=NB * TOPK).then_inc(made2 if k == 0 else made, 1)
            nc.gpsimd.iota(pad[:, :, D:D + 1].bitcast(i32), pattern=[[0, TH], [0, 1]], base=SKIP,
                           channel_multiplier=0).then_inc(made2, 1)
            pool.wait_ge(made, N_MADE)

            def dispatch(i, g, part):
                k = g % RING
                if part[0] == 0:
                    pool.wait_ge(slot_done, count(i, g + 1))
                    pool.wait_ge(dest_done, count(i, g + 1))
                    pool.nop(nofuse=True)
                for n in part:
                    nc.gpsimd.indirect_dma_start(
                        dispatched, bass.IndirectOffsetOnAxis(slot_i[:, k, n:n + 1], 0),
                        rows[:, k, n // TOPK, n % TOPK, :], None).then_inc(scattered[k], 16)

            def step(i, t):
                if has(i, t - 4):
                    dispatch(i, t - 4, (0, 1))
                if has(i, t + 2) or has(i, t - 2):
                    if has(i, t + 2):
                        pool.wait_ge(ve_done[0], count(i, t + 3))
                    if has(i, t - 2):
                        pool.wait_ge(ve_done[1], count(i, t - 1))
                    nc.gpsimd.tensor_tensor(rstd[:, t % RING].rearrange("p a j -> p (a j)"),
                                            ve[:, t % RING].rearrange("p a j -> p (a j)"),
                                            neg_half[:, 0:2 * GB], ALU.pow).then_inc(rstd_done, 1)
                if has(i, t - 4):
                    dispatch(i, t - 4, (2, 3))
                if has(i, t):
                    pool.wait_ge(ms_out, count(i, t + 1))
                    nc.gpsimd.tensor_tensor(rms[:], ms[:], neg_half[:, 0:GB], ALU.pow).then_inc(rms_done, 1)
                if has(i, t - 4):
                    dispatch(i, t - 4, (4, 5, 6, 7))

            pipeline(pool, step, *P1)

            def tile_step(i, t):
                n = t - 1
                if has(i, n, NT):
                    k = n % RING2
                    pool.wait_ge(t_out, count(i, n + 1, 1, RING2))
                    pool.nop(nofuse=True)
                    for a in range(TH):
                        nc.gpsimd.indirect_dma_start(
                            combined, bass.IndirectOffsetOnAxis(tdest[:, k, a:a + 1], 0),
                            tout[:, k, a, :], None, bounds_check=TOK * TOPK - 1, oob_is_err=False)\
                            .then_inc(t_scat[k], 16)

            pipeline(pool, tile_step, *P2, RING2)

            def post_step(i, t):
                g = t - 1
                if has(i, g):
                    k = g % RING
                    pool.wait_ge(p_ve, count(i, g + 1))
                    nc.gpsimd.tensor_tensor(rstd[:, k, 0], ve[:, k, 0], neg_half[:, 0:GB], ALU.pow)\
                        .then_inc(p_rs, 1)
                g = t - 3
                if has(i, g):
                    k = g % RING
                    if g >= RING:
                        pool.wait_ge(p_o, count(i, g - RING + 1))
                        pool.nop(nofuse=True)
                    nc.gpsimd.tensor_tensor(
                        xb3[:, k], xs[:, bass.ds(count(i, g, GB), GB), :],
                        beta_sb[:, :].unsqueeze(1).broadcast_to([P, GB, D]), ALU.add).then_inc(p_xb, 1)
                    pool.wait_ge(p_n, count(i, g + 1))
                    nc.gpsimd.tensor_tensor(g3[:, k], n3[:, k],
                                            gamma_sb[:, :].unsqueeze(1).broadcast_to([P, GB, D]),
                                            ALU.mult).then_inc(p_g, 1)

            pipeline(pool, post_step, *P3)

        @block.tensor
        def _(pe):
            pe.wait_ge(consts, 16 * 10)
            pe.wait_ge(made, N_MADE)
            pe.wait_ge(made2, 4)

            def out_layer(g, graphs):
                if graphs[0] == 0:
                    nc.tensor.matmul(out_ps[:, :], ones_b[0:3, :], b2_parts[:], start=True, stop=False)
                for j in graphs:
                    for c in range(HC):
                        last = nc.tensor.matmul(out_ps[:, j * D:(j + 1) * D],
                                                sbuf_s[:, c, j * P:(j + 1) * P], w2_sb[:, c, :],
                                                start=False, stop=(j == GB - 1 and c == HC - 1))
                return last

            def step(i, t):
                g = t
                if has(i, g):
                    pe.wait_ge(agg_out, count(i, g + 1))
                    for c in range(HC):
                        if g >= 1:
                            pe.wait_ge(z_done, count(i, HC * (g - 1) + c + 1, 1, RING * HC))
                        nc.tensor.matmul(h_ps[c][:, :], w1_sb[:, c * P:(c + 1) * P], agg[:],
                                         start=True, stop=True).then_inc(h_done, 1)
                g = t - 3
                if has(i, g):
                    k = g % RING
                    pe.wait_ge(u_done, count(i, g + 1))
                    if g >= 1:
                        pe.wait_ge(slote_done, count(i, g))
                    for j in range(GB):
                        last = nc.tensor.transpose(misc_ps[:, j * P:(j + 1) * P], rows[:, k, j, 0, 0:D],
                                                   ident[:])
                    last.then_inc(ut_done, 1)
                g = t - 1
                if has(i, g):
                    pe.wait_ge(s_done, count(i, HC * (g + 1), 1, RING * HC))
                    if g >= 1:
                        pe.wait_ge(x1_done, count(i, g))
                    out_layer(g, (0, 1, 2))
                g = t
                if has(i, g):
                    pe.wait_ge(sum_done, count(i, g + 1))
                    for j in range(GB):
                        last = nc.tensor.matmul(agg_ps[:, j:j + 1], sq_sum[:, 2, j * P:(j + 1) * P],
                                                ones_f[:], start=True, stop=True)
                    last.then_inc(ms_done, 1)
                g = t - 3
                if has(i, g):
                    pe.wait_ge(ut_out, count(i, g + 1))
                    for j in range(GB):
                        last = nc.tensor.matmul(misc_ps[:, j * E:(j + 1) * E], ut[:, j * P:(j + 1) * P],
                                                gw_sb[:], start=True, stop=True)
                    last.then_inc(lg_done, 1)
                g = t - 1
                if has(i, g):
                    out_layer(g, (3,)).then_inc(out_done, 1)
                g = t
                if has(i, g):
                    pe.wait_ge(rms_done, count(i, g + 1))
                    for j in range(GB):
                        last = nc.tensor.matmul(rb_ps[:, j * P:(j + 1) * P],
                                                rms[:, j:j + 1].broadcast_to([P, P]), ident[:],
                                                start=True, stop=True)
                    last.then_inc(rb_done, 1)
                g = t + 1
                if has(i, g):
                    k = g % RING
                    pe.wait_ge(loaded[k], count(i, g // RING + 1, 32, 1))
                    pe.wait_ge(xn_done, count(i, g + 1))
                    if g >= 1:
                        pe.wait_ge(ms_out, count(i, g))
                    for j in range(GB):
                        nc.tensor.matmul(agg_ps[:, j * P:(j + 1) * P], xn[:, j, :], adj_sb[:, k, j, :],
                                         start=True, stop=False)
                        last = nc.tensor.matmul(agg_ps[:, j * P:(j + 1) * P], xn[:, j, :], eps_ident[:],
                                                start=False, stop=True)
                    last.then_inc(agg_done, 1)
                g = t - 3
                if has(i, g):
                    k = g % RING
                    pe.wait_ge(cnt_done, count(i, g + 1))
                    if g >= 1:
                        pe.wait_ge(carry_done, count(i, g))
                    wide = lambda a, n: a.unsqueeze(1).broadcast_to([P, n, E])
                    nc.tensor.matmul(misc_ps[:, 0:GB * E], before[:],
                                     cnt[:, k].rearrange("p j e -> p (j e)"), start=True, stop=False)
                    for j in range(GB - 1):
                        nc.tensor.matmul(misc_ps[:, (j + 1) * E:GB * E].rearrange("p (j e) -> p j e", e=E),
                                         ones_b[:], wide(cnt[:, k, j, :], GB - 1 - j), start=False, stop=False)
                    for j in range(GB):
                        last = nc.tensor.matmul(misc_ps[:, 0:GB * E].rearrange("p (j e) -> p j e", e=E),
                                                ones_b[:], wide(carry[:, k, j, :], GB), start=False,
                                                stop=(j == GB - 1))
                    last.then_inc(rank_done, 1)

            pipeline(pe, step, *P1)

            pe.wait_ge(carry_done, NG)
            pe.wait_ge(slote_done, NG)
            for j in range(GB):
                last = nc.tensor.matmul(misc_ps[:, 0:E], ones_b[:], carry[:, NG % RING, j, :],
                                        start=(j == 0), stop=(j == GB - 1))
            last.then_inc(tot_done, 1)

            def tile_step(i, t):
                n = t + 1
                if has(i, n, NT):
                    k = n % RING2
                    pe.wait_ge(tin_in[k], count(i, n // RING2 + 1, 16, 1))
                    if n >= 2:
                        pe.wait_ge(t_ut, count(i, n - 1, 1, RING2))
                    for a in range(TH):
                        last = nc.tensor.transpose(tut_ps[n % 2][:, a * P:(a + 1) * P], tin[:, k, a, 0:D],
                                                   ident[:])
                    last.then_inc(t_tr, 1)
                n = t
                if has(i, n, NT):
                    k = n % RING2
                    pe.wait_ge(wts_in[k], count(i, n // RING2 + 1, 16, 1))
                    pe.wait_ge(t_ut, count(i, n + 1, 1, RING2))
                    if n >= 2:
                        pe.wait_ge(t_relu, count(i, n - 1, 1, RING2))
                    for c in range(FC):
                        last = nc.tensor.matmul(hid_ps[n % 2][:, c * TILE:(c + 1) * TILE],
                                                wts[:, k, c * P:(c + 1) * P], tut[:, n % 2, :],
                                                start=True, stop=True)
                    last.then_inc(t_h, 1)
                n = t - 1
                if has(i, n, NT):
                    k = n % RING2
                    pe.wait_ge(t_relu, count(i, n + 1, 1, RING2))
                    if n >= 2:
                        pe.wait_ge(t_out, count(i, n - 1, 1, RING2))
                    for a in range(TH):
                        for c in range(FC):
                            last = nc.tensor.matmul(exp_ps[n % 2][:, a * D:(a + 1) * D],
                                                    hid[:, n % 2, c, a * P:(a + 1) * P],
                                                    wts[:, k, F + c * D:F + (c + 1) * D],
                                                    start=(c == 0), stop=(c == FC - 1))
                    last.then_inc(t_o, 1)

            pe.wait_ge(x1_done, NG)
            pipeline(pe, tile_step, *P2, RING2)

        @block.scalar
        def _(act):
            def evac_agg(i, g):
                act.wait_ge(agg_done, count(i, g + 1))
                nc.scalar.activation(agg[:], agg_ps[:, :], ACT.Copy).then_inc(agg_out, 1)

            def silu(i, g, c):
                if c == 0 and g >= 1:
                    act.wait_ge(out_done, count(i, g))
                act.wait_ge(z_done, count(i, HC * g + c + 1, 1, RING * HC))
                nc.scalar.activation(sbuf_s[:, c, :], zbuf[:, c, :], ACT.Silu,
                                     scale=rms_sb[:, c:c + 1]).then_inc(s_done, 1)

            def square(i, g, c):
                if g == 0 and i is None and c == 0:
                    act.wait_ge(consts, 16 * 10)
                act.wait_ge(h_done, count(i, HC * g + c + 1, 1, RING * HC))
                nc.scalar.activation(sq[:, c, :], h_ps[c][:, :], ACT.Square, bias=b1_sb[:, c:c + 1])\
                    .then_inc(sq_done, 1)

            def step(i, t):
                if has(i, t - 1):
                    silu(i, t - 1, 0)
                if has(i, t - 1):
                    silu(i, t - 1, 1)
                if has(i, t):
                    evac_agg(i, t)
                if has(i, t - 1):
                    silu(i, t - 1, 2)
                if has(i, t - 1):
                    silu(i, t - 1, 3)
                if has(i, t):
                    square(i, t, 0)
                if has(i, t):
                    square(i, t, 1)
                if has(i, t):
                    square(i, t, 2)
                if has(i, t):
                    square(i, t, 3)
                g = t - 3
                if has(i, g):
                    act.wait_ge(ut_done, count(i, g + 1))
                    nc.scalar.activation(ut[:], misc_ps[:, :], ACT.Copy).then_inc(ut_out, 1)
                g = t + 1
                if has(i, g):
                    k = g % RING
                    act.wait_ge(nb_done[0], count(i, g + 1))
                    if g >= 1:
                        act.wait_ge(agg_done, count(i, g))
                    act.nop(nofuse=True)
                    for j in range(GB):
                        last = nc.scalar.activation(
                            xn[:, j, :], xs[:, bass.ds(count(i, g, GB) + j, 1), :].rearrange("p o d -> p (o d)"),
                            ACT.Identity, bias=nb[:, k, j:j + 1],
                            scale=rstd[:, step_of(0, g) % RING, 0, j:j + 1])
                    last.then_inc(xn_done, 1)
                g = t - 2
                if has(i, g):
                    k = g % RING
                    if g >= RING:
                        act.wait_ge(scattered[k], count(i, g // RING, 16 * GB * TOPK, 1))
                    act.wait_ge(nb_done[1], count(i, g + 1))
                    act.nop(nofuse=True)
                    for j in range(GB):
                        last = nc.scalar.activation(
                            rows[:, k, j, :, 0:D],
                            xs[:, bass.ds(count(i, g, GB) + j, 1), :].broadcast_to([P, TOPK, D]),
                            ACT.Identity, bias=nb_all[:, bass.ds(count(i, g, GB) + j, 1)],
                            scale=rstd[:, t % RING, 1, j:j + 1])
                    last.then_inc(u_done, 1)
                g = t
                if has(i, g):
                    act.wait_ge(rb_done, count(i, g + 1))
                    nc.scalar.activation(rms_b[:], rb_ps[:, :], ACT.Copy).then_inc(rb_out, 1)

            pipeline(act, step, *P1)

            act.wait_ge(pad_done, 1)
            for e in range(E // 2, E):
                r = act.value_load(pad_row[0:1, e:e + 1], min_val=0, max_val=E * CAP)
                act.dma_start(pad_rows(r), pad[:]).then_inc(padded, 16)

            act.wait_ge(gap_done, NG)
            nc.scalar.activation(gw_e[:], gap_all[:], ACT.Exp).then_inc(exp_done, 1)

            def tile_step(i, t):
                n = t
                if has(i, n, NT):
                    k = n % RING2
                    if n >= 2:
                        act.wait_ge(t_o, count(i, n - 1, 1, RING2))
                    act.wait_ge(t_h, count(i, n + 1, 1, RING2))
                    for c in range(FC):
                        last = nc.scalar.activation(
                            hid[:, n % 2, c, :], hid_ps[n % 2][:, c * TILE:(c + 1) * TILE], ACT.Relu,
                            bias=wts[:, k, F + FC * D + c:F + FC * D + c + 1])
                    last.then_inc(t_relu, 1)
                n = t + 4
                if has(i, n, NT):
                    k = n % RING2
                    w = act.value_load(table[0:1, 1, bass.ds(count(i, n, 1, RING2), 1)], min_val=0,
                                       max_val=(E - 1) * P)
                    if n >= RING2:
                        act.wait_ge(t_out, count(i, n - RING2 + 1, 1, RING2))
                    act.dma_start(wts[:, k], w_exp[bass.ds(w, P), :]).then_inc(wts_in[k], 16)

            act.wait_ge(table_done, 1)
            pipeline(act, tile_step, -4, *P2[1:], RING2)

            act.wait_ge(rstd_kept, NG)
            act.wait_ge(nb_done[1], NG)

            def post_step(i, t):
                g = t + 1
                if has(i, g):
                    k = g % RING
                    if g >= RING:
                        act.wait_ge(p_y, count(i, g - RING + 1))
                        act.nop(nofuse=True)
                    for j in range(GB):
                        b = count(i, g, GB) + j
                        last = nc.scalar.activation(
                            u3[:, k, j, :], xs[:, bass.ds(b, 1), :].rearrange("p o d -> p (o d)"),
                            ACT.Identity, bias=nb_all[:, bass.ds(b, 1)], scale=rstd_all[:, bass.ds(b, 1)])
                    last.then_inc(p_u, 1)
                g = t - 2
                if has(i, g):
                    k = g % RING
                    if g >= RING:
                        act.wait_ge(p_g, count(i, g - RING + 1))
                    act.wait_ge(p_nb, count(i, g + 1))
                    act.nop(nofuse=True)
                    for j in range(GB):
                        last = nc.scalar.activation(n3[:, k, j, :], y3[:, k, j, :], ACT.Identity,
                                                    bias=nb[:, k, j:j + 1], scale=rstd[:, k, 0, j:j + 1])
                    last.then_inc(p_n, 1)

            pipeline(act, post_step, *P3)

        @block.vector
        def _(dve):
            dve.wait_ge(made, N_MADE)
            dve.wait_ge(consts, 16 * 10)
            nc.vector.tensor_scalar(eps_ident[:], ident[:], eps_sb[:, 0:1], None, ALU.mult).then_inc(made2, 1)
            n = [0]

            def link(ins):
                n[0] += 1
                ins.then_inc(tab, 1)
                dve.wait_ge(tab, n[0])

            link(nc.vector.tensor_copy(base_e[:], base_i[:]))
            link(nc.vector.tensor_copy(iota_t[:], iota_ti[:]))
            link(nc.vector.tensor_copy(b2_part[:, 0], b2_sb[:]))
            link(nc.vector.tensor_tensor(b2_rest[:, 0], b2_sb[:], b2_part[:, 0], ALU.subtract))
            link(nc.vector.tensor_copy(b2_part[:, 1], b2_rest[:, 0]))
            link(nc.vector.tensor_tensor(b2_rest[:, 1], b2_rest[:, 0], b2_part[:, 1], ALU.subtract))
            link(nc.vector.tensor_copy(b2_part[:, 2], b2_rest[:, 1]))
            link(nc.vector.tensor_scalar(b2_row[:, 0], b2_part[:, 0], ident[0:3, 0:1], None, ALU.mult))
            for k in (1, 2):
                link(nc.vector.scalar_tensor_tensor(out=b2_row[:, k], in0=b2_part[:, k],
                                                    scalar=ident[0:3, k:k + 1], in1=b2_row[:, k - 1],
                                                    op0=ALU.mult, op1=ALU.add))
            nc.vector.tensor_copy(b2_parts[:].rearrange("p (j d) -> p j d", d=D),
                                  b2_row[:, 2:3, :].broadcast_to([3, GB, D])).then_inc(made2, 1)

            def variance(ln, i, g):
                k = g % RING
                dve.wait_ge(bn_done[ln], count(i, g + 1))
                dve.nop(nofuse=True)
                for j in range(GB):
                    last = nc.vector.bn_aggr(mv[:, ln, k, j, :], bn[:, ln, k, j, :])
                last.then_inc(mv_done[ln], 1)

            def variance_eps(ln, i, g):
                k = g % RING
                dve.wait_ge(mv_done[ln], count(i, g + 1))
                nc.vector.tensor_scalar(ve[:, step_of(ln, g) % RING, ln], mv[:, ln, k, :, 1], LN_EPS, None,
                                        ALU.add).then_inc(ve_done[ln], 1)

            def offset(ln, i, g):
                k = g % RING
                dve.wait_ge(rstd_done, count(i, step_of(ln, g) + 3))
                to = nb[:, k] if ln == 0 else nb_all[:, bass.ds(count(i, g, GB), GB)]
                if ln == 1:
                    dve.nop(nofuse=True)
                nc.vector.scalar_tensor_tensor(out=to, in0=mv[:, ln, k, :, 0], scalar=-1.0,
                                               in1=rstd[:, step_of(ln, g) % RING, ln], op0=ALU.mult,
                                               op1=ALU.mult).then_inc(nb_done[ln], 1)
                if ln == 1:
                    nc.vector.tensor_copy(rstd_all[:, bass.ds(count(i, g, GB), GB)],
                                          rstd[:, step_of(ln, g) % RING, ln]).then_inc(rstd_kept, 1)

            def step(i, t):
                g = t - 2
                if has(i, g):
                    k = g % RING
                    x1 = xs[:, bass.ds(count(i, g, GB), GB), :]
                    dve.wait_ge(out_done, count(i, g + 1))
                    nc.vector.tensor_tensor(x1, out_ps[:, :].rearrange("p (b d) -> p b d", d=D), x1,
                                            ALU.add).then_inc(x1_done, 1)
                    dve.wait_ge(x1_done, count(i, g + 1))
                    dve.nop(nofuse=True)
                    for j in range(GB):
                        last = nc.vector.bn_stats(bn[:, 1, k, j, :], xs[:, bass.ds(count(i, g, GB) + j, 1), :])
                    last.then_inc(bn_done[1], 1)
                g = t + 2
                if has(i, g):
                    k = g % RING
                    dve.wait_ge(loaded[k], count(i, g // RING + 1, 32, 1))
                    dve.nop(nofuse=True)
                    for j in range(GB):
                        last = nc.vector.bn_stats(bn[:, 0, k, j, :], xs[:, bass.ds(count(i, g, GB) + j, 1), :])
                    last.then_inc(bn_done[0], 1)
                if has(i, t - 2):
                    variance(1, i, t - 2)
                if has(i, t + 2):
                    variance(0, i, t + 2)
                if has(i, t - 2):
                    variance_eps(1, i, t - 2)
                if has(i, t + 2):
                    variance_eps(0, i, t + 2)
                g = t
                if has(i, g):
                    for n in range(2):
                        dve.wait_ge(sq_done, count(i, HC * g + 2 * n + 2, 1, RING * HC))
                        nc.vector.tensor_tensor(sq_sum[:, n, :], sq[:, 2 * n, :], sq[:, 2 * n + 1, :], ALU.add)\
                            .then_inc(half_done, 1)
                    dve.wait_ge(half_done, count(i, 2 * g + 2, 1, 2 * RING))
                    nc.vector.tensor_tensor(sq_sum[:, 2, :], sq_sum[:, 0, :], sq_sum[:, 1, :], ALU.add)\
                        .then_inc(sum_done, 1)
                if has(i, t - 2):
                    offset(1, i, t - 2)
                if has(i, t + 2):
                    offset(0, i, t + 2)
                g = t
                if has(i, g):
                    dve.wait_ge(ms_done, count(i, g + 1))
                    nc.vector.tensor_scalar(ms[:], agg_ps[:, 0:GB], 1.0 / H, RMS_EPS, ALU.mult, ALU.add)\
                        .then_inc(ms_out, 1)
                g = t - 3
                if has(i, g):
                    k = g % RING
                    dve.wait_ge(lg_done, count(i, g + 1))
                    nc.vector.tensor_tensor(lgs[:], misc_ps[:, 0:GB * E].rearrange("p (j e) -> p j e", e=E),
                                            gb_sb[:, :].unsqueeze(1).broadcast_to([P, GB, E]), ALU.add)\
                        .then_inc(lg_out, 1)
                    dve.wait_ge(lg_out, count(i, g + 1))
                    dve.nop(nofuse=True)
                    for j in range(GB):
                        last = nc.vector.max(top_v[:, j, :], lgs[:, j, :])
                    last.then_inc(topv_done, 1)
                    dve.wait_ge(topv_done, count(i, g + 1))
                    dve.nop(nofuse=True)
                    for j in range(GB):
                        last = nc.vector.max_index(top_i[:, j, :], top_v[:, j, :], lgs[:, j, :])
                    last.then_inc(topi_done, 1)
                    nc.vector.tensor_tensor(gap_all[:, bass.ds(count(i, g, GB), GB)], top_v[:, :, 1],
                                            top_v[:, :, 0], ALU.subtract).then_inc(gap_done, 1)
                    dve.wait_ge(topi_done, count(i, g + 1))
                    for c in range(TOPK):
                        last = nc.vector.tensor_tensor(
                            hot[:, :, c, :], iota_e[:, :].unsqueeze(1).broadcast_to([P, GB, E]),
                            top_i[:, :, c:c + 1].broadcast_to([P, GB, E]), ALU.is_equal)
                    last.then_inc(hot_done, 1)
                    dve.wait_ge(hot_done, count(i, g + 1))
                    nc.vector.tensor_tensor(cnt[:, k], hot[:, :, 0, :], hot[:, :, 1, :], ALU.add)\
                        .then_inc(cnt_done, 1)
                    dve.wait_ge(cnt_done, count(i, g + 1))
                    nc.vector.tensor_tensor(carry[:, (k + 1) % RING], carry[:, k], cnt[:, k], ALU.add)\
                        .then_inc(carry_done, 1)
                g = t
                if has(i, g):
                    dve.wait_ge(rb_out, count(i, g + 1))
                    for c in range(HC):
                        nc.vector.scalar_tensor_tensor(out=zbuf[:, c, :], in0=h_ps[c][:, :],
                                                       scalar=b1_sb[:, c:c + 1], in1=rms_b[:],
                                                       op0=ALU.add, op1=ALU.mult).then_inc(z_done, 1)
                g = t - 3
                if has(i, g):
                    k = g % RING
                    dve.wait_ge(rank_done, count(i, g + 1))
                    nc.vector.tensor_tensor(slot_e[:], misc_ps[:, 0:GB * E].rearrange("p (j e) -> p j e", e=E),
                                            base_e[:, :].unsqueeze(1).broadcast_to([P, GB, E]), ALU.add)\
                        .then_inc(slote_done, 1)
                    dve.wait_ge(slote_done, count(i, g + 1))
                    for c in range(TOPK):
                        last = nc.vector.tensor_tensor(slot_m[:, :, c, :], hot[:, :, c, :], slot_e[:], ALU.mult)
                    last.then_inc(slotm_done, 1)
                    if g >= RING:
                        dve.wait_ge(scattered[k], count(i, g // RING, 16 * GB * TOPK, 1))
                    dest = rows[:, k, :, :, D:D + 1].bitcast(i32).rearrange("p b c o -> p (b c) o")
                    nc.vector.tensor_scalar(dest, dest, float(RING * GB * TOPK), None, ALU.add)\
                        .then_inc(dest_done, 1)
                    dve.wait_ge(slotm_done, count(i, g + 1))
                    nc.vector.tensor_reduce(slot_f[:], slot_m[:].rearrange("p j c e -> p (j c) e"),
                                            axis=AX.X, op=ALU.add).then_inc(slotf_done, 1)
                    dve.wait_ge(slotf_done, count(i, g + 1))
                    nc.vector.tensor_copy(slot_i[:, k, :], slot_f[:]).then_inc(slot_done, 1)

            pipeline(dve, step, *P1)

            dve.wait_ge(tot_done, 1)
            link(nc.vector.tensor_copy(tot[:], misc_ps[:, 0:E]))
            nc.vector.tensor_tensor(pad_row[:], base_e[0:1, :], tot[0:1, :], ALU.add).then_inc(pad_done, 1)
            link(nc.vector.tensor_scalar(nt_i[:, 0, :], tot[:], float(TILE - 1), None, ALU.add))
            link(nc.vector.tensor_single_scalar(nt_i[:, 1, :], nt_i[:, 0, :], TILE.bit_length() - 1,
                                                op=ALU.arith_shift_right))
            link(nc.vector.tensor_copy(nt_f[:], nt_i[:, 1, :]))
            link(nc.vector.tensor_tensor(nt_m[:], upto[:], nt_f[:, :].unsqueeze(1).broadcast_to([P, E, E]),
                                         ALU.mult))
            link(nc.vector.tensor_reduce(end_t[:], nt_m[:], axis=AX.X, op=ALU.add))
            link(nc.vector.tensor_tensor(t_m[:], end_t[0:1, :].unsqueeze(1).broadcast_to([1, NT, E]),
                                         iota_t[:, :].unsqueeze(2).broadcast_to([1, NT, E]), ALU.is_le))
            link(nc.vector.tensor_reduce(t_e[:], t_m[:], axis=AX.X, op=ALU.add))
            link(nc.vector.tensor_tensor(t_n[:], t_m[:], nt_f[0:1, :].unsqueeze(1).broadcast_to([1, NT, E]),
                                         ALU.mult))
            link(nc.vector.tensor_reduce(t_s[:], t_n[:], axis=AX.X, op=ALU.add))
            link(nc.vector.tensor_tensor(t_r[:, 0], iota_t[:], t_s[:], ALU.subtract))
            link(nc.vector.tensor_scalar(t_r[:, 1], t_e[:], float(CAP), None, ALU.mult))
            link(nc.vector.scalar_tensor_tensor(out=t_r[:, 2], in0=t_r[:, 0], scalar=float(TILE),
                                                in1=t_r[:, 1], op0=ALU.mult, op1=ALU.add))
            link(nc.vector.tensor_scalar(table[:, 0], t_r[:, 2], float(E * CAP), None, ALU.min))
            nc.vector.tensor_scalar(table[:, 1], t_e[:], float(E - 1), float(P), ALU.min, ALU.mult)\
                .then_inc(table_done, 1)

            dve.wait_ge(exp_done, 1)
            link(nc.vector.tensor_scalar(gw_d[:], gw_e[:], 1.0, None, ALU.add))
            link(nc.vector.reciprocal(gate[:, 0, :], gw_d[:]))
            link(nc.vector.tensor_tensor(gate[:, 1, :], gw_e[:], gate[:, 0, :], ALU.mult))

            def tile_step(i, t):
                n = t + 1
                if has(i, n, NT):
                    dve.wait_ge(t_tr, count(i, n + 1, 1, RING2))
                    if n >= 2:
                        dve.wait_ge(t_h, count(i, n - 1, 1, RING2))
                    nc.vector.tensor_copy(tut[:, n % 2, :], tut_ps[n % 2][:, 0:TILE]).then_inc(t_ut, 1)
                n = t - 1
                if has(i, n, NT):
                    k = n % RING2
                    if n >= RING2:
                        dve.wait_ge(t_scat[k], count(i, n // RING2, 16 * TH, 1))
                    nc.vector.tensor_copy(tdest[:, k], tin[:, k, :, D:D + 1].bitcast(i32)
                                          .rearrange("p a o -> p (a o)"))
                    dve.wait_ge(t_o, count(i, n + 1, 1, RING2))
                    nc.vector.tensor_tensor(
                        tout[:, k], exp_ps[n % 2][:, 0:TH * D].rearrange("p (a d) -> p a d", d=D),
                        wts[:, k, WROW - D:WROW].unsqueeze(1).broadcast_to([P, TH, D]), ALU.add)\
                        .then_inc(t_out, 1)

            pipeline(dve, tile_step, *P2, RING2)

            def weighted(i, g, c, dst):
                k = g % RING
                for j in range(GB):
                    last = nc.vector.scalar_tensor_tensor(
                        out=dst[:, k, j, :], in0=moe[:, k, j, c, :],
                        scalar=gate[:, c, bass.ds(count(i, g, GB) + j, 1)],
                        in1=u3[:, k, j, :], op0=ALU.mult, op1=ALU.add)
                return last

            def post_step(i, t):
                g = t - 2
                if has(i, g):
                    k = g % RING
                    dve.wait_ge(p_rs, count(i, g + 1))
                    nc.vector.scalar_tensor_tensor(out=nb[:, k], in0=mv[:, 0, k, :, 0], scalar=-1.0,
                                                   in1=rstd[:, k, 0], op0=ALU.mult, op1=ALU.mult)\
                        .then_inc(p_nb, 1)
                g = t
                if has(i, g):
                    k = g % RING
                    dve.wait_ge(p_u, count(i, g + 1))
                    dve.wait_ge(moe_in[k], count(i, g // RING + 1, 16, 1))
                    weighted(i, g, 0, u3).then_inc(p_y1, 1)
                g = t - 1
                if has(i, g):
                    k = g % RING
                    dve.wait_ge(p_bn, count(i, g + 1))
                    dve.nop(nofuse=True)
                    for j in range(GB):
                        last = nc.vector.bn_aggr(mv[:, 0, k, j, :], bn[:, 0, k, j, :])
                    last.then_inc(p_mv, 1)
                g = t
                if has(i, g):
                    if g >= RING:
                        dve.wait_ge(p_n, count(i, g - RING + 1))
                    dve.wait_ge(p_y1, count(i, g + 1))
                    weighted(i, g, 1, y3).then_inc(p_y, 1)
                g = t - 1
                if has(i, g):
                    k = g % RING
                    dve.wait_ge(p_mv, count(i, g + 1))
                    nc.vector.tensor_scalar(ve[:, k, 0], mv[:, 0, k, :, 1], LN_EPS, None, ALU.add)\
                        .then_inc(p_ve, 1)
                g = t - 4
                if has(i, g):
                    k = g % RING
                    if g >= RING:
                        dve.wait_ge(stored[k], count(i, g // RING, 16, 1))
                    dve.wait_ge(p_xb, count(i, g + 1))
                    dve.wait_ge(p_g, count(i, g + 1))
                    nc.vector.tensor_tensor(o3[:, k], g3[:, k], xb3[:, k], ALU.add).then_inc(p_o, 1)
                g = t
                if has(i, g):
                    k = g % RING
                    dve.wait_ge(p_y, count(i, g + 1))
                    for j in range(GB):
                        last = nc.vector.bn_stats(bn[:, 0, k, j, :], y3[:, k, j, :])
                    last.then_inc(p_bn, 1)

            pipeline(dve, post_step, *P3)


def kernel(**inputs):
    import numpy as np
    import concourse.bacc as bacc
    from concourse.bass_utils import run_bass_kernel_spmd

    a = {k: np.asarray(v) for k, v in inputs.items()}
    col = lambda v, n: np.ascontiguousarray(v.reshape(n, P).T)
    w_exp = np.concatenate([
        a["L0_ffn_w1"],
        a["L0_ffn_w2"].reshape(E, FC, P, D).transpose(0, 2, 1, 3).reshape(E, P, FC * D),
        a["L0_ffn_b1"].reshape(E, FC, P).transpose(0, 2, 1),
        np.broadcast_to(a["L0_ffn_b2"][:, None, :], (E, P, D)),
    ], axis=2).reshape(E * P, WROW)
    arrays = {
        "x": a["x"].transpose(1, 0, 2),
        "adj_t": a["adj"].transpose(2, 0, 1),
        "eps": a["L0_gnn_epsilon"].reshape(1),
        "w1": a["L0_gnn_W1"], "b1": col(a["L0_gnn_b1"], HC), "rms_w": col(a["L0_gnn_rms_weight"], HC),
        "w2": a["L0_gnn_W2"].reshape(HC, P, D).transpose(1, 0, 2), "b2": a["L0_gnn_b2"],
        "gate_w": a["L0_ffn_gate_w"], "gate_b": a["L0_ffn_gate_b"],
        "w_exp": w_exp, "gamma": a["L0_ffn_gamma"], "beta": a["L0_ffn_beta"],
    }
    arrays = {k: np.ascontiguousarray(v) for k, v in arrays.items()}
    nc = bacc.Bacc("TRN2", target_bir_lowering=False, num_devices=1)
    args = [nc.dram_tensor(f"in_{k}", v.shape, mybir.dt.from_np(v.dtype), kind="ExternalInput").ap()
            for k, v in arrays.items()]
    out = nc.dram_tensor("out_0", (P, NB, D), mybir.dt.float32, kind="ExternalOutput").ap()
    gnn_moe(nc, *args, out)
    r = run_bass_kernel_spmd(nc, [{f"in_{k}": v for k, v in arrays.items()}], core_ids=[0])
    return np.ascontiguousarray(r.results[0]["out_0"].transpose(1, 0, 2))
```
